# Optimizing a Trainium2 kernel written in Bass

```python
import numpy as np
import jax
import jax.numpy as jnp

def _softmax(x, axis=-1):
    return jax.nn.softmax(x, axis=axis)

def _gelu(x):
    return jax.nn.gelu(x, approximate=True)

def _silu(x):
    return jax.nn.silu(x)

def _sigmoid(x):
    return jax.nn.sigmoid(x)

def _layernorm(x, axis=-1, eps=1e-05):
    m = jnp.mean(x, axis=axis, keepdims=True)
    v = jnp.var(x, axis=axis, keepdims=True)
    return (x - m) / jnp.sqrt(v + eps)

def _scatter_add(tgt, idx, src, axis=0):
    return tgt.at[idx].add(src)

def _segment_sum(src, seg, n):
    return jax.ops.segment_sum(src, seg, n)
kernel_name = 'mk_cond_seq_d4_seqx_r4_31fcd0'

def setup_inputs(seed: int=0):
    np.random.seed(seed)
    _w = jnp.asarray

    def _rec_inputs():
        import jax
        import jax.numpy as jnp
        _rk = jax.random.key(seed)
        x = 7.22e-05 + 1 * jax.random.normal(jax.random.fold_in(_rk, 1), (16, 256, 256), jnp.float32)
        _lenS = 256 - jax.random.randint(jax.random.fold_in(_rk, 7), (16,), 0, max(1, 256 // 4) + 1, jnp.int32)
        _lenS2 = 256 - jax.random.randint(jax.random.fold_in(_rk, 8), (16,), 0, max(1, 256 // 4) + 1, jnp.int32)
        cond_2048 = 0.00782532 + 1.00527 * jax.random.normal(jax.random.fold_in(_rk, 11), (16, 512), jnp.float32)
        _validS = jnp.arange(256)[None, :] < _lenS[:, None]
        _validS2 = jnp.arange(256)[None, :] < _lenS2[:, None]
        _causal = jnp.tril(jnp.ones((256, 256), dtype=bool))
        mask_BxSx1_fk1 = jnp.where(jnp.ones((16, 256, 1), dtype=bool), 1.0, 0.0).astype(jnp.float32)
        mask_BxS_ff1 = jnp.where(jnp.ones((16, 256), dtype=bool), 1.0, 0.0).astype(jnp.float32)
        mask_BxS_ik0 = jnp.where(jnp.broadcast_to(_validS[:, :], (16, 256)), 0, 1).astype(jnp.int32)
        return (x, cond_2048, mask_BxSx1_fk1, mask_BxS_ff1, mask_BxS_ik0)
    x, cond_2048, mask_BxSx1_fk1, mask_BxS_ff1, mask_BxS_ik0 = _rec_inputs()

    def _L0_cond_setup():
        import jax, jax.numpy as jnp
        import numpy as np
        B, T, D, H, TE = (4, 512, 256, 8, 512)
        EPS = 1e-05

        def _ln(x, w, b):
            m = jnp.mean(x, axis=-1, keepdims=True)
            v = jnp.mean((x - m) ** 2, axis=-1, keepdims=True)
            return (x - m) * jax.lax.rsqrt(v + EPS) * w + b
        key = jax.random.key(seed)
        ks = jax.random.split(key, 16)
        s = 0.02
        inp = {'x': jax.random.normal(ks[0], (B, T, D), jnp.float32), 'emb': jax.random.normal(ks[1], (B, TE), jnp.float32), 'src_mask': (jax.random.uniform(ks[2], (B, T, 1)) > 0.2).astype(jnp.float32), 'num_head': H, 'ln_w': jnp.ones((D,), jnp.float32), 'ln_b': jnp.zeros((D,), jnp.float32), 'Wq': jax.random.normal(ks[3], (D, D), jnp.float32) * s, 'bq': jnp.zeros((D,), jnp.float32), 'Wk': jax.random.normal(ks[4], (D, D), jnp.float32) * s, 'bk': jnp.zeros((D,), jnp.float32), 'Wv': jax.random.normal(ks[5], (D, D), jnp.float32) * s, 'bv': jnp.zeros((D,), jnp.float32), 'W_emb': jax.random.normal(ks[6], (TE, 2 * D), jnp.float32) * s, 'b_emb': jnp.zeros((2 * D,), jnp.float32), 'ln2_w': jnp.ones((D,), jnp.float32), 'ln2_b': jnp.zeros((D,), jnp.float32), 'W_out': jax.random.normal(ks[7], (D, D), jnp.float32) * s, 'b_out': jnp.zeros((D,), jnp.float32)}
        return inp
    _L0_cond_all = _L0_cond_setup()
    _L0_cond_in = {k: v for k, v in _L0_cond_all.items() if k in ('ln_w', 'ln_b', 'Wq', 'bq', 'Wk', 'bk', 'Wv', 'bv', 'W_emb', 'b_emb', 'ln2_w', 'ln2_b', 'W_out', 'b_out')}
    del _L0_cond_all

    def _L1_cond_setup():
        import jax, jax.numpy as jnp
        import numpy as np
        B, T, D, H, TE = (8, 256, 256, 16, 512)
        LN_EPS = 1e-05

        def layer_norm(x, w, b):
            m = jnp.mean(x, axis=-1, keepdims=True)
            v = jnp.var(x, axis=-1, keepdims=True)
            return (x - m) / jnp.sqrt(v + LN_EPS) * w + b
        key = jax.random.key(seed)
        ks = jax.random.split(key, 8)
        s = lambda k, sh: jax.random.normal(k, sh, jnp.float32) * 0.02
        return dict(x=jax.random.normal(ks[0], (B, T, D), jnp.float32), emb=jax.random.normal(ks[1], (B, TE), jnp.float32), src_mask=jnp.ones((B, T), jnp.float32), norm_w=jnp.ones((D,), jnp.float32), norm_b=jnp.zeros((D,), jnp.float32), q_w=s(ks[2], (D, D)), q_b=jnp.zeros((D,), jnp.float32), k_w=s(ks[3], (D, D)), k_b=jnp.zeros((D,), jnp.float32), v_w=s(ks[4], (D, D)), v_b=jnp.zeros((D,), jnp.float32), emb_w=s(ks[5], (TE, 2 * D)), emb_b=jnp.zeros((2 * D,), jnp.float32), sb_norm_w=jnp.ones((D,), jnp.float32), sb_norm_b=jnp.zeros((D,), jnp.float32), out_w=s(ks[6], (D, D)), out_b=jnp.zeros((D,), jnp.float32))
    _L1_cond_all = _L1_cond_setup()
    _L1_cond_in = {k: v for k, v in _L1_cond_all.items() if k in ('norm_w', 'norm_b', 'q_w', 'q_b', 'k_w', 'k_b', 'v_w', 'v_b', 'emb_w', 'emb_b', 'sb_norm_w', 'sb_norm_b', 'out_w', 'out_b')}
    del _L1_cond_all

    def _L2_cond_setup():
        import jax, jax.numpy as jnp
        import numpy as np
        H = 16
        LN_EPS = 1e-05

        def _layernorm(x, scale, bias):
            mu = jnp.mean(x, axis=-1, keepdims=True)
            var = jnp.var(x, axis=-1, keepdims=True)
            return (x - mu) * jax.lax.rsqrt(var + LN_EPS) * scale + bias
        key = jax.random.key(seed)
        ks = jax.random.split(key, 8)
        B, T, D, E = (4, 1024, 256, 512)
        s = 0.02
        return {'x': jax.random.normal(ks[0], (B, T, D), jnp.float32), 'emb': jax.random.normal(ks[1], (B, E), jnp.float32), 'src_mask': jax.random.randint(ks[2], (B, T), 0, 2).astype(jnp.int32), 'norm_scale': jnp.ones((D,), jnp.float32), 'norm_bias': jnp.zeros((D,), jnp.float32), 'Wq': jax.random.normal(ks[3], (D, D), jnp.float32) * s, 'bq': jnp.zeros((D,), jnp.float32), 'Wk': jax.random.normal(ks[4], (D, D), jnp.float32) * s, 'bk': jnp.zeros((D,), jnp.float32), 'Wv': jax.random.normal(ks[5], (D, D), jnp.float32) * s, 'bv': jnp.zeros((D,), jnp.float32), 'film_emb_W': jax.random.normal(ks[6], (E, 2 * D), jnp.float32) * s, 'film_emb_b': jnp.zeros((2 * D,), jnp.float32), 'film_norm_scale': jnp.ones((D,), jnp.float32), 'film_norm_bias': jnp.zeros((D,), jnp.float32), 'film_out_W': jax.random.normal(ks[7], (D, D), jnp.float32) * s, 'film_out_b': jnp.zeros((D,), jnp.float32)}
    _L2_cond_all = _L2_cond_setup()
    _L2_cond_in = {k: v for k, v in _L2_cond_all.items() if k in ('norm_scale', 'norm_bias', 'Wq', 'bq', 'Wk', 'bk', 'Wv', 'bv', 'film_emb_W', 'film_emb_b', 'film_norm_scale', 'film_norm_bias', 'film_out_W', 'film_out_b')}
    del _L2_cond_all

    def _L3_cond_setup():
        import jax, jax.numpy as jnp
        import numpy as np
        D = 256
        DI = 512
        N = 16
        DT_RANK = 64
        D_CONV = 4
        EPS = 1e-05

        def _layernorm(x, g, b):
            mu = jnp.mean(x, axis=-1, keepdims=True)
            var = jnp.mean((x - mu) ** 2, axis=-1, keepdims=True)
            return (x - mu) * jax.lax.rsqrt(var + EPS) * g + b

        def _mamba(xn, in_proj_w, conv_w, conv_b, x_proj_w, dt_proj_w, dt_proj_b, A_log, D_param, out_proj_w):
            b, sl, _ = xn.shape
            xz = jnp.einsum('bsd,ed->bse', xn, in_proj_w)
            x_in, z = jnp.split(xz, 2, axis=-1)
            xt = jnp.transpose(x_in, (0, 2, 1))
            u = jax.lax.conv_general_dilated(xt, conv_w[:, None, :], (1,), [(D_CONV - 1, 0)], feature_group_count=DI, dimension_numbers=('NCH', 'OIH', 'NCH')) + conv_b[None, :, None]
            u = jax.nn.silu(jnp.transpose(u, (0, 2, 1)))
            x_dbl = jnp.einsum('bsd,ed->bse', u, x_proj_w)
            dt_r, B, C = jnp.split(x_dbl, [DT_RANK, DT_RANK + N], axis=-1)
            dt = jax.nn.softplus(jnp.einsum('bsr,dr->bsd', dt_r, dt_proj_w) + dt_proj_b)
            A = -jnp.exp(A_log)

            def step(h, inp):
                dt_t, B_t, C_t, u_t = inp
                dA = jnp.exp(dt_t[:, :, None] * A)
                h = h * dA + (dt_t * u_t)[:, :, None] * B_t[:, None, :]
                y = jnp.einsum('bdn,bn->bd', h, C_t)
                return (h, y)
            seq = (jnp.transpose(dt, (1, 0, 2)), jnp.transpose(B, (1, 0, 2)), jnp.transpose(C, (1, 0, 2)), jnp.transpose(u, (1, 0, 2)))
            h0 = jnp.zeros((b, DI, N), xn.dtype)
            _, ys = jax.lax.scan(step, h0, seq)
            y = jnp.transpose(ys, (1, 0, 2)) + u * D_param
            y = y * jax.nn.silu(z)
            return jnp.einsum('bsd,ed->bse', y, out_proj_w)
        key = jax.random.key(seed)
        ks = jax.random.split(key, 16)
        s = lambda fan: 1.0 / np.sqrt(fan)
        inp = {'x': jax.random.normal(ks[0], (2, 512, D), jnp.float32), 'c': jax.random.normal(ks[1], (2, 2 * D), jnp.float32), 'ln_g': jnp.ones((D,), jnp.float32), 'ln_b': jnp.zeros((D,), jnp.float32), 'ada_w': jax.random.normal(ks[2], (3 * D, 2 * D), jnp.float32) * s(2 * D), 'ada_b': jnp.zeros((3 * D,), jnp.float32), 'in_proj_w': jax.random.normal(ks[3], (2 * DI, D), jnp.float32) * s(D), 'conv_w': jax.random.normal(ks[4], (DI, D_CONV), jnp.float32) * s(D_CONV), 'conv_b': jnp.zeros((DI,), jnp.float32), 'x_proj_w': jax.random.normal(ks[5], (DT_RANK + 2 * N, DI), jnp.float32) * s(DI), 'dt_proj_w': jax.random.normal(ks[6], (DI, DT_RANK), jnp.float32) * s(DT_RANK), 'dt_proj_b': jax.random.uniform(ks[7], (DI,), jnp.float32, -4.0, -2.0), 'A_log': jnp.tile(jnp.log(jnp.arange(1, N + 1, dtype=jnp.float32)), (DI, 1)), 'D_param': jnp.ones((DI,), jnp.float32), 'out_proj_w': jax.random.normal(ks[8], (D, DI), jnp.float32) * s(DI)}
        return inp
    _L3_cond_all = _L3_cond_setup()
    _L3_cond_in = {k: v for k, v in _L3_cond_all.items() if k in ('ln_g', 'ln_b', 'ada_w', 'ada_b', 'in_proj_w', 'conv_w', 'conv_b', 'x_proj_w', 'dt_proj_w', 'dt_proj_b', 'A_log', 'D_param', 'out_proj_w')}
    del _L3_cond_all
    return {'x': x, 'cond_2048': cond_2048, 'mask_BxSx1_fk1': mask_BxSx1_fk1, 'mask_BxS_ff1': mask_BxS_ff1, 'mask_BxS_ik0': mask_BxS_ik0, 'L0_cond_ln_w': _L0_cond_in['ln_w'], 'L0_cond_ln_b': _L0_cond_in['ln_b'], 'L0_cond_Wq': _L0_cond_in['Wq'], 'L0_cond_bq': _L0_cond_in['bq'], 'L0_cond_Wk': _L0_cond_in['Wk'], 'L0_cond_bk': _L0_cond_in['bk'], 'L0_cond_Wv': _L0_cond_in['Wv'], 'L0_cond_bv': _L0_cond_in['bv'], 'L0_cond_W_emb': _L0_cond_in['W_emb'], 'L0_cond_b_emb': _L0_cond_in['b_emb'], 'L0_cond_ln2_w': _L0_cond_in['ln2_w'], 'L0_cond_ln2_b': _L0_cond_in['ln2_b'], 'L0_cond_W_out': _L0_cond_in['W_out'], 'L0_cond_b_out': _L0_cond_in['b_out'], 'L1_cond_norm_w': _L1_cond_in['norm_w'], 'L1_cond_norm_b': _L1_cond_in['norm_b'], 'L1_cond_q_w': _L1_cond_in['q_w'], 'L1_cond_q_b': _L1_cond_in['q_b'], 'L1_cond_k_w': _L1_cond_in['k_w'], 'L1_cond_k_b': _L1_cond_in['k_b'], 'L1_cond_v_w': _L1_cond_in['v_w'], 'L1_cond_v_b': _L1_cond_in['v_b'], 'L1_cond_emb_w': _L1_cond_in['emb_w'], 'L1_cond_emb_b': _L1_cond_in['emb_b'], 'L1_cond_sb_norm_w': _L1_cond_in['sb_norm_w'], 'L1_cond_sb_norm_b': _L1_cond_in['sb_norm_b'], 'L1_cond_out_w': _L1_cond_in['out_w'], 'L1_cond_out_b': _L1_cond_in['out_b'], 'L2_cond_norm_scale': _L2_cond_in['norm_scale'], 'L2_cond_norm_bias': _L2_cond_in['norm_bias'], 'L2_cond_Wq': _L2_cond_in['Wq'], 'L2_cond_bq': _L2_cond_in['bq'], 'L2_cond_Wk': _L2_cond_in['Wk'], 'L2_cond_bk': _L2_cond_in['bk'], 'L2_cond_Wv': _L2_cond_in['Wv'], 'L2_cond_bv': _L2_cond_in['bv'], 'L2_cond_film_emb_W': _L2_cond_in['film_emb_W'], 'L2_cond_film_emb_b': _L2_cond_in['film_emb_b'], 'L2_cond_film_norm_scale': _L2_cond_in['film_norm_scale'], 'L2_cond_film_norm_bias': _L2_cond_in['film_norm_bias'], 'L2_cond_film_out_W': _L2_cond_in['film_out_W'], 'L2_cond_film_out_b': _L2_cond_in['film_out_b'], 'L3_cond_ln_g': _L3_cond_in['ln_g'], 'L3_cond_ln_b': _L3_cond_in['ln_b'], 'L3_cond_ada_w': _L3_cond_in['ada_w'], 'L3_cond_ada_b': _L3_cond_in['ada_b'], 'L3_cond_in_proj_w': _L3_cond_in['in_proj_w'], 'L3_cond_conv_w': _L3_cond_in['conv_w'], 'L3_cond_conv_b': _L3_cond_in['conv_b'], 'L3_cond_x_proj_w': _L3_cond_in['x_proj_w'], 'L3_cond_dt_proj_w': _L3_cond_in['dt_proj_w'], 'L3_cond_dt_proj_b': _L3_cond_in['dt_proj_b'], 'L3_cond_A_log': _L3_cond_in['A_log'], 'L3_cond_D_param': _L3_cond_in['D_param'], 'L3_cond_out_proj_w': _L3_cond_in['out_proj_w']}

def reference(x, cond_2048, mask_BxSx1_fk1, mask_BxS_ff1, mask_BxS_ik0, L0_cond_ln_w, L0_cond_ln_b, L0_cond_Wq, L0_cond_bq, L0_cond_Wk, L0_cond_bk, L0_cond_Wv, L0_cond_bv, L0_cond_W_emb, L0_cond_b_emb, L0_cond_ln2_w, L0_cond_ln2_b, L0_cond_W_out, L0_cond_b_out, L1_cond_norm_w, L1_cond_norm_b, L1_cond_q_w, L1_cond_q_b, L1_cond_k_w, L1_cond_k_b, L1_cond_v_w, L1_cond_v_b, L1_cond_emb_w, L1_cond_emb_b, L1_cond_sb_norm_w, L1_cond_sb_norm_b, L1_cond_out_w, L1_cond_out_b, L2_cond_norm_scale, L2_cond_norm_bias, L2_cond_Wq, L2_cond_bq, L2_cond_Wk, L2_cond_bk, L2_cond_Wv, L2_cond_bv, L2_cond_film_emb_W, L2_cond_film_emb_b, L2_cond_film_norm_scale, L2_cond_film_norm_bias, L2_cond_film_out_W, L2_cond_film_out_b, L3_cond_ln_g, L3_cond_ln_b, L3_cond_ada_w, L3_cond_ada_b, L3_cond_in_proj_w, L3_cond_conv_w, L3_cond_conv_b, L3_cond_x_proj_w, L3_cond_dt_proj_w, L3_cond_dt_proj_b, L3_cond_A_log, L3_cond_D_param, L3_cond_out_proj_w):
    import jax
    import jax.numpy as jnp

    def _L0_cond_ref(x, emb, src_mask, num_head, ln_w, ln_b, Wq, bq, Wk, bk, Wv, bv, W_emb, b_emb, ln2_w, ln2_b, W_out, b_out):
        import jax, jax.numpy as jnp
        import numpy as np
        B, T, D, H, TE = (4, 512, 256, 8, 512)
        EPS = 1e-05

        def _ln(x, w, b):
            m = jnp.mean(x, axis=-1, keepdims=True)
            v = jnp.mean((x - m) ** 2, axis=-1, keepdims=True)
            return (x - m) * jax.lax.rsqrt(v + EPS) * w + b
        b, t, d = x.shape
        h = num_head
        dh = d // h
        xn = _ln(x, ln_w, ln_b)
        q = xn @ Wq + bq
        k = xn @ Wk + bk + (1.0 - src_mask) * -1000000.0
        q = jax.nn.softmax(q.reshape(b, t, h, dh), axis=-1)
        k = jax.nn.softmax(k.reshape(b, t, h, dh), axis=1)
        v = ((xn @ Wv + bv) * src_mask).reshape(b, t, h, dh)
        att = jnp.einsum('bnhd,bnhl->bhdl', k, v)
        y = jnp.einsum('bnhd,bhdl->bnhl', q, att).reshape(b, t, d)
        emb_out = (jax.nn.silu(emb) @ W_emb + b_emb)[:, None, :]
        scale, shift = jnp.split(emb_out, 2, axis=2)
        hh = _ln(y, ln2_w, ln2_b) * (1.0 + scale) + shift
        hh = jax.nn.silu(hh) @ W_out + b_out
        return x + hh

    def _L1_cond_ref(x, emb, src_mask, norm_w, norm_b, q_w, q_b, k_w, k_b, v_w, v_b, emb_w, emb_b, sb_norm_w, sb_norm_b, out_w, out_b):
        import jax, jax.numpy as jnp
        import numpy as np
        B, T, D, H, TE = (8, 256, 256, 16, 512)
        LN_EPS = 1e-05

        def layer_norm(x, w, b):
            m = jnp.mean(x, axis=-1, keepdims=True)
            v = jnp.var(x, axis=-1, keepdims=True)
            return (x - m) / jnp.sqrt(v + LN_EPS) * w + b
        Bx, Tx, Dx = x.shape
        xn = layer_norm(x, norm_w, norm_b)
        q = (xn @ q_w + q_b).reshape(Bx, Tx, H, -1)
        k = (xn @ k_w + k_b).reshape(Bx, Tx, H, -1)
        att = jnp.einsum('bnhl,bmhl->bnmh', q, k)
        mask = src_mask.reshape(Bx, 1, Tx, 1)
        att = att + (1.0 - mask) * -1000000.0
        att = jax.nn.softmax(att, axis=2)
        v = ((xn @ v_w + v_b) * src_mask[:, :, None]).reshape(Bx, Tx, H, -1)
        y = jnp.einsum('bnmh,bmhl->bnhl', att, v).reshape(Bx, Tx, Dx)
        e = jax.nn.silu(emb) @ emb_w + emb_b
        scale, shift = jnp.split(e[:, None, :], 2, axis=2)
        h = layer_norm(y, sb_norm_w, sb_norm_b) * (1.0 + scale) + shift
        h = jax.nn.silu(h) @ out_w + out_b
        return x + h

    def _L2_cond_ref(x, emb, src_mask, norm_scale, norm_bias, Wq, bq, Wk, bk, Wv, bv, film_emb_W, film_emb_b, film_norm_scale, film_norm_bias, film_out_W, film_out_b):
        import jax, jax.numpy as jnp
        import numpy as np
        H = 16
        LN_EPS = 1e-05

        def _layernorm(x, scale, bias):
            mu = jnp.mean(x, axis=-1, keepdims=True)
            var = jnp.var(x, axis=-1, keepdims=True)
            return (x - mu) * jax.lax.rsqrt(var + LN_EPS) * scale + bias
        B, T, D = x.shape
        dh = D // H
        xn = _layernorm(x, norm_scale, norm_bias)
        q = xn @ Wq + bq
        k = xn @ Wk + bk
        v = xn @ Wv + bv
        mask = (src_mask == 1)[:, :, None]
        k = jnp.where(mask, -jnp.inf, k)
        v = jnp.where(mask, 0.0, v)
        q = q.reshape(B, T, H, dh).transpose(0, 2, 1, 3)
        k = k.reshape(B, T, H, dh).transpose(0, 2, 1, 3)
        v = v.reshape(B, T, H, dh).transpose(0, 2, 1, 3)
        q = jax.nn.softmax(q, axis=-1)
        k = jax.nn.softmax(k, axis=2)
        attn = jnp.einsum('bhse,bhsd->bhed', k, v)
        y = jnp.einsum('bhtd,bhed->bhte', q, attn)
        y = y.transpose(0, 2, 1, 3).reshape(B, T, D)
        emb_out = jax.nn.silu(emb) @ film_emb_W + film_emb_b
        scale, shift = jnp.split(emb_out, 2, axis=-1)
        h = _layernorm(y, film_norm_scale, film_norm_bias) * (1.0 + scale[:, None, :]) + shift[:, None, :]
        h = jax.nn.silu(h) @ film_out_W + film_out_b
        return x + h

    def _L3_cond_ref(x, c, ln_g, ln_b, ada_w, ada_b, in_proj_w, conv_w, conv_b, x_proj_w, dt_proj_w, dt_proj_b, A_log, D_param, out_proj_w):
        import jax, jax.numpy as jnp
        import numpy as np
        D = 256
        DI = 512
        N = 16
        DT_RANK = 64
        D_CONV = 4
        EPS = 1e-05

        def _layernorm(x, g, b):
            mu = jnp.mean(x, axis=-1, keepdims=True)
            var = jnp.mean((x - mu) ** 2, axis=-1, keepdims=True)
            return (x - mu) * jax.lax.rsqrt(var + EPS) * g + b

        def _mamba(xn, in_proj_w, conv_w, conv_b, x_proj_w, dt_proj_w, dt_proj_b, A_log, D_param, out_proj_w):
            b, sl, _ = xn.shape
            xz = jnp.einsum('bsd,ed->bse', xn, in_proj_w)
            x_in, z = jnp.split(xz, 2, axis=-1)
            xt = jnp.transpose(x_in, (0, 2, 1))
            u = jax.lax.conv_general_dilated(xt, conv_w[:, None, :], (1,), [(D_CONV - 1, 0)], feature_group_count=DI, dimension_numbers=('NCH', 'OIH', 'NCH')) + conv_b[None, :, None]
            u = jax.nn.silu(jnp.transpose(u, (0, 2, 1)))
            x_dbl = jnp.einsum('bsd,ed->bse', u, x_proj_w)
            dt_r, B, C = jnp.split(x_dbl, [DT_RANK, DT_RANK + N], axis=-1)
            dt = jax.nn.softplus(jnp.einsum('bsr,dr->bsd', dt_r, dt_proj_w) + dt_proj_b)
            A = -jnp.exp(A_log)

            def step(h, inp):
                dt_t, B_t, C_t, u_t = inp
                dA = jnp.exp(dt_t[:, :, None] * A)
                h = h * dA + (dt_t * u_t)[:, :, None] * B_t[:, None, :]
                y = jnp.einsum('bdn,bn->bd', h, C_t)
                return (h, y)
            seq = (jnp.transpose(dt, (1, 0, 2)), jnp.transpose(B, (1, 0, 2)), jnp.transpose(C, (1, 0, 2)), jnp.transpose(u, (1, 0, 2)))
            h0 = jnp.zeros((b, DI, N), xn.dtype)
            _, ys = jax.lax.scan(step, h0, seq)
            y = jnp.transpose(ys, (1, 0, 2)) + u * D_param
            y = y * jax.nn.silu(z)
            return jnp.einsum('bsd,ed->bse', y, out_proj_w)
        ada = jnp.einsum('bc,ec->be', jax.nn.silu(c), ada_w) + ada_b
        shift, scale, gate = jnp.split(ada, 3, axis=1)
        xn = _layernorm(x, ln_g, ln_b)
        xn = xn * (1.0 + scale[:, None, :]) + shift[:, None, :]
        x_ssm = _mamba(xn, in_proj_w, conv_w, conv_b, x_proj_w, dt_proj_w, dt_proj_b, A_log, D_param, out_proj_w)
        return x + gate[:, None, :] * x_ssm
    x = _L0_cond_ref(x, cond_2048, mask_BxSx1_fk1, 8, L0_cond_ln_w, L0_cond_ln_b, L0_cond_Wq, L0_cond_bq, L0_cond_Wk, L0_cond_bk, L0_cond_Wv, L0_cond_bv, L0_cond_W_emb, L0_cond_b_emb, L0_cond_ln2_w, L0_cond_ln2_b, L0_cond_W_out, L0_cond_b_out)
    x = _L1_cond_ref(x, cond_2048, mask_BxS_ff1, L1_cond_norm_w, L1_cond_norm_b, L1_cond_q_w, L1_cond_q_b, L1_cond_k_w, L1_cond_k_b, L1_cond_v_w, L1_cond_v_b, L1_cond_emb_w, L1_cond_emb_b, L1_cond_sb_norm_w, L1_cond_sb_norm_b, L1_cond_out_w, L1_cond_out_b)
    x = _L2_cond_ref(x, cond_2048, mask_BxS_ik0, L2_cond_norm_scale, L2_cond_norm_bias, L2_cond_Wq, L2_cond_bq, L2_cond_Wk, L2_cond_bk, L2_cond_Wv, L2_cond_bv, L2_cond_film_emb_W, L2_cond_film_emb_b, L2_cond_film_norm_scale, L2_cond_film_norm_bias, L2_cond_film_out_W, L2_cond_film_out_b)
    x = _L3_cond_ref(x, cond_2048, L3_cond_ln_g, L3_cond_ln_b, L3_cond_ada_w, L3_cond_ada_b, L3_cond_in_proj_w, L3_cond_conv_w, L3_cond_conv_b, L3_cond_x_proj_w, L3_cond_dt_proj_w, L3_cond_dt_proj_b, L3_cond_A_log, L3_cond_D_param, L3_cond_out_proj_w)
    return x

_drawn_inputs = setup_inputs


def setup_inputs(seed=0):
    import zlib

    import numpy as np

    out = dict(_drawn_inputs(seed))
    spreads = {'L0_cond_ln_w': (1.0, 0.6),
     'L0_cond_ln_b': (0.0, 0.1),
     'L0_cond_bq': (0.0, 0.8),
     'L0_cond_bk': (0.0, 0.8),
     'L0_cond_bv': (0.0, 0.1),
     'L0_cond_b_emb': (0.0, 0.1),
     'L0_cond_ln2_w': (1.0, 0.2),
     'L0_cond_ln2_b': (0.0, 0.395),
     'L0_cond_b_out': (0.0, 0.1),
     'L1_cond_norm_w': (1.0, 0.2),
     'L1_cond_norm_b': (0.0, 0.1),
     'L1_cond_q_b': (0.0, 0.8),
     'L1_cond_k_b': (0.0, 0.8),
     'L1_cond_v_b': (0.0, 0.1),
     'L1_cond_emb_b': (0.0, 0.1),
     'L1_cond_sb_norm_w': (1.0, 0.2),
     'L1_cond_sb_norm_b': (0.0, 0.341),
     'L1_cond_out_b': (0.0, 0.1),
     'L2_cond_norm_scale': (1.0, 0.534),
     'L2_cond_norm_bias': (0.0, 0.1),
     'L2_cond_bq': (0.0, 0.446),
     'L2_cond_bk': (0.0, 0.8),
     'L2_cond_bv': (0.0, 0.1),
     'L2_cond_film_emb_b': (0.0, 0.312),
     'L2_cond_film_norm_scale': (1.0, 0.2),
     'L2_cond_film_norm_bias': (0.0, 0.364),
     'L2_cond_film_out_b': (0.0, 0.1),
     'L3_cond_ln_g': (1.0, 0.2),
     'L3_cond_ln_b': (0.0, 0.1),
     'L3_cond_ada_b': (0.0, 0.1),
     'L3_cond_conv_b': (0.0, 0.1),
     'L3_cond_D_param': (1.0, 0.2)}
    factors = {'L0_cond_Wq': 8.0, 'L0_cond_Wk': 8.0, 'L2_cond_Wk': 4.302}
    for name, (base, spread) in spreads.items():
        noise = np.random.default_rng([zlib.crc32(name.encode()), seed]).standard_normal(out[name].shape)
        drawn = base * np.exp(spread * noise) if base else spread * noise
        out[name] = jnp.asarray(drawn.astype(out[name].dtype))
    for name, factor in factors.items():
        out[name] = (out[name] * factor).astype(out[name].dtype)
    return out
```

```python
from contextlib import ExitStack

import concourse.bass as bass
from concourse import mybir

F32 = mybir.dt.float32
BF16 = mybir.dt.bfloat16
I32 = mybir.dt.int32
ALU = mybir.AluOpType
ACT = mybir.ActivationFunctionType
AX = mybir.AxisListType

P = 128
B, T, D = 16, 256, 256
E = 512
PAIR = 2 * T
TT = PAIR // P
FT = D // P
PAIRS = B // 2
LANES = 2
STEPS = PAIRS // LANES
EPS = 1e-5


class Signal:

    def __init__(self, sem, per=1, start=0):
        self.sem, self.per, self.start = sem, per, start

    def nth(self, step, n=1):
        return step * self.per + n + self.start


class Chain:

    def __init__(self, sem, per):
        self.sem, self.per = sem, per

    def begin(self, eng, step):
        self.eng, self.step, self.n = eng, step, 0

    def link(self, ins):
        self.n += 1
        assert self.n <= self.per
        ins.then_inc(self.sem, 1)
        self.eng.wait_ge(self.sem, self.step * self.per + self.n)

    def end(self):
        assert self.n == self.per, (self.n, self.per)


def wait(eng, signal, step, n=1):
    eng.wait_ge(signal.sem, signal.nth(step, n))


def layer_semaphore(nc, used, name):
    used.append(nc.alloc_semaphore(name=name))
    return used[-1]


def release_semaphores(nc, used):
    nc.all_engine_barrier()
    nc.clear_and_free_semaphores(used)
    nc.all_engine_barrier()


def row_tiles(dram):
    return dram.rearrange("b (h p) d -> p (b h) d", p=P)


def k_tiles(dram):
    return dram.rearrange("(k p) n -> p k n", p=P)


def setup(nc, a, keep):
    used = []
    with ExitStack() as ctx:
        def sb(name, shape, dt=F32):
            return ctx.enter_context(nc.sbuf_tensor(name, shape, dt))

        def ps(name, shape, dt=F32):
            return ctx.enter_context(nc.psum_tensor(name, shape, dt))

        def sem(name):
            return layer_semaphore(nc, used, name)

        KE = E // P
        cond = sb("cond", [P, KE, B])
        cond_act = sb("cond_act", [P, KE, B])
        emb_w = [sb(f"emb_w{l}", [P, KE, 2 * D]) for l in range(3)] + [sb("emb_w3", [P, KE, 3 * D])]
        emb_b = [sb(f"emb_b{l}", [P, 2 * FT]) for l in range(4)]
        emb = [sb(f"emb{l}", [P, 2 * FT, B]) for l in range(4)]
        gain = [sb(f"gain{l}", [P, FT, B]) for l in range(4)]
        ln_w = [sb(f"mod_w{l}", [P, FT]) for l in range(4)]
        ln_b = [sb(f"mod_b{l}", [P, FT]) for l in range(4)]
        gate_b = sb("gate_b", [B, D])
        gate = sb("gate", [B, D])
        emb_ps = [ps(f"emb_ps{l}", [P, 2 * FT, B]) for l in range(4)]
        gate_ps = ps("gate_ps", [B, D])
        cond_in, vec_in, x_in = (sem(s) for s in ("cond_in", "vec_in", "x_in"))
        emb_ins = [sem(f"emb_in{l}") for l in range(4)]
        cond_ready, emb_done, gate_done, gate_ready, gate_out, made = (
            sem(s) for s in ("cond_ready", "emb_done", "gate_done", "gate_ready", "gate_out", "made"))

        with nc.Block() as block:
            @block.sync
            def _(sp):
                sp.dma_start(cond[:], k_tiles(a["cond_t"])).then_inc(cond_in, 16)
                xt = row_tiles(a["x"])
                for l in range(4):
                    sp.dma_start(emb_w[l][:], k_tiles(a["emb_w"][l])).then_inc(emb_ins[l], 16)
                sp.dma_start(keep["x"][:, 0:LANES * TT, :], xt[:, 0:LANES * TT, :]).then_inc(x_in, 16)
                for u in range(LANES, PAIRS):
                    sp.dma_start(keep["x"][:, u * TT:(u + 1) * TT, :], xt[:, u * TT:(u + 1) * TT, :])\
                      .then_inc(keep["x_rest_in"], 16)
                sp.wait_ge(gate_ready, 1)
                sp.dma_start(a["gate_dram"], gate[:]).then_inc(gate_out, 16)
                sp.wait_ge(gate_out, 16)
                sp.wait_ge(x_in, 16)

            @block.gpsimd
            def _(pool):
                pool.memset(keep["half"][:], -0.5).then_inc(made, 1)
                pool.memset(keep["eps"][:], EPS).then_inc(made, 1)
                pool.memset(keep["ident"][:], 0.0).then_inc(made, 1)
                pool.wait_ge(made, 3)
                pool.affine_select(out=keep["ident"][:], in_=keep["ident"][:], compare_op=ALU.not_equal, fill=1.0,
                                   base=0, pattern=[[-1, P]], channel_multiplier=1).then_inc(made, 1)
                for l in range(3):
                    for dst, src in keep["loads"][l]:
                        pool.dma_start(dst, src).then_inc(keep["w_in"][l], 16)

            @block.scalar
            def _(act):
                for l in range(4):
                    act.dma_start(emb_b[l][:], a["emb_b"][l][:, 0:2 * FT]).then_inc(vec_in, 16)
                    act.dma_start(ln_w[l][:], a["mod_w"][l]).then_inc(vec_in, 16)
                    act.dma_start(ln_b[l][:], a["mod_b"][l]).then_inc(vec_in, 16)
                act.dma_start(gate_b[:], a["gate_b"].partition_broadcast(B)).then_inc(vec_in, 16)
                act.wait_ge(cond_in, 16)
                act.activation(cond_act[:], cond[:], ACT.Silu).then_inc(cond_ready, 1)

            @block.tensor
            def _(pe):
                pe.wait_ge(cond_ready, 1)
                for l in range(4):
                    pe.wait_ge(emb_ins[l], 16)
                    for m in range(2 * FT):
                        for k in range(KE):
                            last = pe.matmul(emb_ps[l][:, m, :], emb_w[l][:, k, m * P:(m + 1) * P], cond_act[:, k, :],
                                             start=(k == 0), stop=(k == KE - 1))
                    last.then_inc(emb_done, 1)
                for k in range(KE):
                    last = pe.matmul(gate_ps[:], cond_act[:, k, :], emb_w[3][:, k, 2 * D:3 * D],
                                     start=(k == 0), stop=(k == KE - 1))
                last.then_inc(gate_done, 1)

            @block.vector
            def _(dve):
                chain = Chain(sem("setup_chain"), 4 * 3)
                chain.begin(dve, 0)
                dve.wait_ge(vec_in, 16 * 13)
                for l in range(4):
                    shift, scale = (slice(0, FT), slice(FT, 2 * FT)) if l == 3 else (slice(FT, 2 * FT), slice(0, FT))
                    dve.wait_ge(emb_done, l + 1)
                    chain.link(dve.tensor_tensor(emb[l][:], emb_ps[l][:],
                                                 emb_b[l][:].unsqueeze(2).broadcast_to([P, 2 * FT, B]), ALU.add))
                    chain.link(dve.tensor_scalar(gain[l][:], emb[l][:, scale, :], 1.0, None, ALU.add))
                    dve.tensor_tensor(keep["mod_scale"][l][:], gain[l][:],
                                      ln_w[l][:].unsqueeze(2).broadcast_to([P, FT, B]), ALU.mult)
                    chain.link(dve.tensor_tensor(gain[l][:], gain[l][:],
                                                 ln_b[l][:].unsqueeze(2).broadcast_to([P, FT, B]), ALU.mult))
                    dve.tensor_tensor(keep["mod_shift"][l][:], gain[l][:], emb[l][:, shift, :], ALU.add)
                chain.end()
                dve.wait_ge(gate_done, 1)
                dve.tensor_tensor(gate[:], gate_ps[:], gate_b[:], ALU.add).then_inc(gate_ready, 1)
    release_semaphores(nc, used)


def layer_norm_stats(dve, src, stats, mean_var, done):
    for t in range(TT):
        dve.bn_stats(stats[:, t, :], src(t))
    dve.drain()
    for t in range(TT):
        last = dve.bn_aggr(mean_var[:, t, :], stats[:, t, :])
    last.then_inc(done.sem, 1)


def layer_norm_rstd(pool, chain, keep, mean_var, rstd, done):
    chain.link(pool.tensor_tensor(rstd[:], mean_var[:, :, 1], keep["eps"][:], ALU.add))
    pool.tensor_tensor(rstd[:], rstd[:], keep["half"][:], ALU.pow).then_inc(done.sem, 1)


def layer_norm_apply(dve, src, dst, mean_var, rstd, done):
    for t in range(TT):
        last = dve.tensor_scalar(dst[:, t, :], src(t), mean_var[:, t, 0:1], rstd[:, t:t + 1],
                                 ALU.subtract, ALU.mult)
    last.then_inc(done.sem, 1)


def transpose_rows(pe, keep, out, rows, done):
    for f in range(FT):
        for t in range(TT):
            last = pe.transpose(out[:, f, t * P:(t + 1) * P], rows[:, t, f * P:(f + 1) * P], keep["ident"][:])
    last.then_inc(done.sem, 1)


def project_rows(pe, out, feats, w, done, tiles=FT):
    for t in range(TT):
        for k in range(tiles):
            last = pe.matmul(out[:, t, :], feats[:, k, t * P:(t + 1) * P], w[:, k, :],
                             start=(k == 0), stop=(k == tiles - 1))
    last.then_inc(done.sem, 1)


def project_feats(pe, out, feats, w, done):
    for m in range(FT):
        for k in range(FT):
            last = pe.matmul(out[:, m, :], w[:, k, m * P:(m + 1) * P], feats[:, k, :],
                             start=(k == 0), stop=(k == FT - 1))
    last.then_inc(done.sem, 1)


def silu_modulated(act, keep, l, pair, src, dst, done):
    for f in range(FT):
        for b in range(2):
            e = pair * 2 + b
            last = act.activation(dst[:, f, b * T:(b + 1) * T], src[:, f, b * T:(b + 1) * T], ACT.Silu,
                                  bias=keep["mod_shift"][l][:, f, bass.ds(e, 1)],
                                  scale=keep["mod_scale"][l][:, f, bass.ds(e, 1)])
    last.then_inc(done.sem, 1)


def linear_attention(nc, a, keep, l, heads):
    dh = D // heads
    masked_if_one = l == 2
    v_first = l == 2
    used = []
    with ExitStack() as ctx:
        def sb(name, shape, dt=F32):
            return ctx.enter_context(nc.sbuf_tensor(f"{name}_l{l}", shape, dt))

        def ps(name, shape, dt=F32):
            return ctx.enter_context(nc.psum_tensor(f"{name}_l{l}", shape, dt))

        def sem(name):
            return layer_semaphore(nc, used, f"{name}_l{l}")

        def lanes(name, shape, dt=F32):
            return [sb(f"{name}{p}", shape, dt) for p in range(LANES)]

        def signals(name, per=1, start=0):
            return [Signal(sem(f"{name}{p}"), per, start) for p in range(LANES)]

        w, weights_in = keep["w"][l], 16 * len(keep["loads"][l])
        mask_dt = I32 if masked_if_one else F32
        mask_raw = sb("mask_raw", [P, B * T], mask_dt)
        mask_bias = lanes("mask_bias", [P, PAIR])
        keep_raw = sb("keep_raw", [P, PAIRS * TT], mask_dt)
        keep_row = sb("keep_row", [P, PAIRS * TT])
        block_mask = sb("block_mask", [P, P])

        stats = lanes("stats", [P, TT, 6])
        mean_var = lanes("mean_var", [P, TT, 2])
        rstd = lanes("rstd", [P, TT])
        rows = lanes("rows", [P, TT, D])
        feats = lanes("feats", [P, FT, PAIR])
        k_feats = lanes("k_feats", [P, FT, PAIR])
        k_negmax = lanes("k_negmax", [P, 2 * FT])
        k_sum = lanes("k_sum", [P, 2 * FT])
        k_rows = lanes("k_rows", [P, TT, D])
        v_rows = lanes("v_rows", [P, TT, D])
        q_rows = lanes("q_rows", [P, TT, D])
        q_max = lanes("q_max", [P, TT * heads])
        q_rsum = lanes("q_rsum", [P, TT * heads])
        q_feats = lanes("q_feats", [P, FT, PAIR])
        att = lanes("att", [P, 2 * FT, P])
        y = lanes("y", [P, TT, D])

        bank_a = [ps(f"bank_a{p}", [P, 2 * 512]) for p in range(LANES)]
        bank_b = [ps(f"bank_b{p}", [P, 2 * 512]) for p in range(LANES)]

        def by_feat(x):
            return x[:].rearrange("p (f t) -> p f t", f=FT)

        def by_row(x):
            return x[:].rearrange("p (t f) -> p t f", t=TT)

        def by_head(x):
            return x[:].rearrange("p t (h e) -> p (t h) e", e=dh)

        mask_in, keep_in, masks_made, blocks_made = (sem(s) for s in ("mask_in", "keep_in", "masks_made", "blocks_made"))
        x_stats, x_rstd, x_normed = signals("x_stats"), signals("x_rstd"), signals("x_normed")
        x_turned, feats_ready = signals("x_turned"), signals("feats_ready")
        k_done, k_masked, k_exp = signals("k_done"), signals("k_masked"), signals("k_exp")
        k_normed = signals("k_normed")
        k_turned, k_ready = signals("k_turned"), signals("k_ready")
        q_done, q_read, q_shifted, q_exp = signals("q_done"), signals("q_read"), signals("q_shifted"), signals("q_exp")
        q_turned, q_ready = signals("q_turned"), signals("q_ready")
        v_done, v_ready = signals("v_done"), signals("v_ready")
        att_done, att_ready, y_done = signals("att_done"), signals("att_ready"), signals("y_done")
        y_stats, y_rstd, y_normed = signals("y_stats"), signals("y_rstd"), signals("y_normed")
        h_turned, h_ready, out_done, x_ready = signals("h_turned"), signals("h_ready"), signals("out_done"), signals("x_ready", start=1)
        dve_chain = [Chain(sem(f"dve_chain{p}"), 8) for p in range(LANES)]
        pool_chain = [Chain(sem(f"pool_chain{p}"), 2) for p in range(LANES)]

        with nc.Block() as block:
            @block.sync
            def _(sp):
                mask = a["mask"][l]
                sp.dma_start(mask_raw[:], mask.rearrange("b t -> (b t)").partition_broadcast(P)).then_inc(mask_in, 16)
                sp.dma_start(keep_raw[:], a["mask_rows"][l]).then_inc(keep_in, 16)
                sp.wait_ge(mask_in, 16)
                sp.wait_ge(keep_in, 16)

            @block.gpsimd
            def _(pool):
                n = 0
                pool.memset(block_mask[:], 1.0).then_inc(blocks_made, 1)
                view = block_mask[:].rearrange("p (h e) -> p h e", e=dh)
                pool.wait_ge(blocks_made, 1)
                pool.affine_select(out=view, in_=view, compare_op=ALU.is_ge, fill=0.0, base=0,
                                   pattern=[[-dh, P // dh], [0, dh]], channel_multiplier=1).then_inc(blocks_made, 1)
                pool.wait_ge(blocks_made, 2)
                pool.affine_select(out=view, in_=view, compare_op=ALU.is_ge, fill=0.0, base=dh - 1,
                                   pattern=[[dh, P // dh], [0, dh]], channel_multiplier=-1).then_inc(blocks_made, 1)
                with pool.Fori(0, STEPS) as i:
                    for p in range(LANES):
                        pool_chain[p].begin(pool, i)
                        wait(pool, x_stats[p], i)
                        layer_norm_rstd(pool, pool_chain[p], keep, mean_var[p], rstd[p], x_rstd[p])
                    for p in range(LANES):
                        wait(pool, y_stats[p], i)
                        layer_norm_rstd(pool, pool_chain[p], keep, mean_var[p], rstd[p], y_rstd[p])
                        pool_chain[p].end()

            @block.tensor
            def _(pe):
                pe.wait_ge(keep["w_in"][l], weights_in)
                with pe.Fori(0, STEPS) as i:
                    for p in range(LANES):
                        wait(pe, x_normed[p], i)
                        wait(pe, x_ready[p], i, 0)
                        transpose_rows(pe, keep, by_feat(bank_a[p]), rows[p], x_turned[p])
                    for p in range(LANES):
                        wait(pe, feats_ready[p], i)
                        project_feats(pe, by_feat(bank_b[p]), feats[p], w["k"], k_done[p])
                    for p in range(LANES):
                        project_rows(pe, by_row(bank_a[p]), feats[p], w["q"], q_done[p])
                    for p in range(LANES):
                        wait(pe, k_normed[p] if v_first else k_exp[p], i)
                        for t in range(TT):
                            for f in range(FT):
                                last = pe.transpose(by_row(bank_b[p])[:, t, f * P:(f + 1) * P],
                                                    k_feats[p][:, f, t * P:(t + 1) * P], keep["ident"][:])
                        last.then_inc(k_turned[p].sem, 1)
                    for p in range(LANES):
                        wait(pe, q_read[p], i)
                        project_rows(pe, by_row(bank_a[p]), feats[p], w["v"], v_done[p])
                    for p in range(LANES):
                        wait(pe, q_exp[p], i)
                        wait(pe, k_ready[p], i)
                        transpose_rows(pe, keep, by_feat(bank_b[p]), q_rows[p], q_turned[p])
                    att_w, att_x = (v_rows, k_rows) if v_first else (k_rows, v_rows)
                    for p in range(LANES):
                        wait(pe, v_ready[p], i)
                        for b in range(2):
                            for f in range(FT):
                                for t in range(2):
                                    last = pe.matmul(bank_a[p][:, (b * FT + f) * P:(b * FT + f + 1) * P],
                                                     att_w[p][:, 2 * b + t, f * P:(f + 1) * P],
                                                     att_x[p][:, 2 * b + t, f * P:(f + 1) * P],
                                                     start=(t == 0), stop=(t == 1))
                        last.then_inc(att_done[p].sem, 1)
                    for p in range(LANES):
                        wait(pe, att_ready[p], i)
                        wait(pe, q_ready[p], i)
                        for t in range(TT):
                            for f in range(FT):
                                last = pe.matmul(by_row(bank_b[p])[:, t, f * P:(f + 1) * P],
                                                 q_feats[p][:, f, t * P:(t + 1) * P], att[p][:, (t // 2) * FT + f, :],
                                                 start=True, stop=True)
                        last.then_inc(y_done[p].sem, 1)
                    for p in range(LANES):
                        wait(pe, y_normed[p], i)
                        transpose_rows(pe, keep, by_feat(bank_a[p]), rows[p], h_turned[p])
                    for p in range(LANES):
                        wait(pe, h_ready[p], i)
                        project_rows(pe, by_row(bank_b[p]), feats[p], w["out"], out_done[p])

            @block.scalar
            def _(act):
                act.wait_ge(keep["w_in"][l], weights_in)
                with act.Fori(0, STEPS) as i:
                    for p in range(LANES):
                        wait(act, x_turned[p], i)
                        for f in range(FT):
                            last = act.activation(feats[p][:, f, :], by_feat(bank_a[p])[:, f, :], ACT.Identity,
                                                  bias=w["ln_b"][:, f:f + 1], scale=w["ln_w"][:, f:f + 1])
                        last.then_inc(feats_ready[p].sem, 1)
                    for p in range(LANES):
                        wait(act, k_masked[p], i)
                        for f in range(FT):
                            for b in range(2):
                                c = f * 2 + b
                                part = k_feats[p][:, f, b * T:(b + 1) * T]
                                last = act.activation(part, part, ACT.Exp, bias=k_negmax[p][:, c:c + 1],
                                                      accum_out=k_sum[p][:, c:c + 1])
                        last.then_inc(k_exp[p].sem, 1)
                    for p in range(LANES):
                        wait(act, q_shifted[p], i)
                        act.activation(q_rows[p][:], q_rows[p][:], ACT.Exp).then_inc(q_exp[p].sem, 1)
                    for p in range(LANES):
                        wait(act, k_turned[p], i)
                        act.activation(k_rows[p][:], by_row(bank_b[p]), ACT.Copy).then_inc(k_ready[p].sem, 1)
                    for p in range(LANES):
                        wait(act, q_turned[p], i)
                        act.activation(q_feats[p][:], by_feat(bank_b[p]), ACT.Copy).then_inc(q_ready[p].sem, 1)
                    for p in range(LANES):
                        wait(act, h_turned[p], i)
                        silu_modulated(act, keep, l, i * LANES + p, by_feat(bank_a[p]), feats[p], h_ready[p])

            @block.vector
            def _(dve):
                dve.wait_ge(keep_in, 16)
                if masked_if_one:
                    dve.tensor_scalar(keep_row[:], keep_raw[:], 1.0, None, ALU.not_equal).then_inc(masks_made, 1)
                else:
                    dve.tensor_copy(keep_row[:], keep_raw[:]).then_inc(masks_made, 1)
                dve.wait_ge(masks_made, 1)
                dve.wait_ge(blocks_made, 3)
                dve.wait_ge(mask_in, 16)
                for p in range(LANES):
                    dve.sem_inc(x_ready[p].sem, 1)
                dve.wait_ge(keep["w_in"][l], weights_in)
                dve.wait_ge(keep["x_rest_in"], 16 * (PAIRS - LANES))
                with dve.Fori(0, STEPS) as i:
                    def x_tile(p):
                        return lambda t: keep["x"][:, bass.ds((i * LANES + p) * TT + t, 1), :].rearrange("p a d -> p (a d)")

                    def x_pair(p):
                        return keep["x"][:, bass.ds((i * LANES + p) * TT, TT), :]

                    for p in range(LANES):
                        dve_chain[p].begin(dve, i)
                        layer_norm_stats(dve, x_tile(p), stats[p], mean_var[p], x_stats[p])
                    for p in range(LANES):
                        raw = mask_raw[:, bass.ds((i * LANES + p) * PAIR, PAIR)]
                        if masked_if_one:
                            dve.tensor_scalar(mask_bias[p][:], raw, 1.0, -1e30, ALU.is_equal, ALU.mult)
                        else:
                            dve.tensor_scalar(mask_bias[p][:], raw, 1.0, 1e6, ALU.subtract, ALU.mult)
                        wait(dve, x_rstd[p], i)
                        layer_norm_apply(dve, x_tile(p), rows[p], mean_var[p], rstd[p], x_normed[p])
                    for p in range(LANES):
                        wait(dve, k_done[p], i)
                        for f in range(FT):
                            last = dve.scalar_tensor_tensor(k_feats[p][:, f, :], by_feat(bank_b[p])[:, f, :],
                                                            w["bk"][:, f:f + 1], mask_bias[p][:], ALU.add, ALU.add)
                        dve_chain[p].link(last)
                        dve.tensor_reduce(k_negmax[p][:], k_feats[p][:].rearrange("p f (b t) -> p (f b) t", b=2),
                                          AX.X, ALU.max, negate=True).then_inc(k_masked[p].sem, 1)
                    for p in range(LANES):
                        wait(dve, q_done[p], i)
                        dve.tensor_tensor(q_rows[p][:], by_row(bank_a[p]),
                                          w["bq"][:].unsqueeze(1).broadcast_to([P, TT, D]), ALU.add)\
                           .then_inc(q_read[p].sem, 1)
                        wait(dve, q_read[p], i)
                        dve_chain[p].link(dve.tensor_reduce(q_max[p][:], by_head(q_rows[p]), AX.X, ALU.max))
                        dve.tensor_tensor(by_head(q_rows[p]), by_head(q_rows[p]),
                                          q_max[p][:].unsqueeze(2).broadcast_to([P, TT * heads, dh]), ALU.subtract)\
                           .then_inc(q_shifted[p].sem, 1)
                    if v_first:
                        for p in range(LANES):
                            wait(dve, k_exp[p], i)
                            dve_chain[p].link(dve.reciprocal(k_sum[p][:], k_sum[p][:]))
                            for c in range(2 * FT):
                                part = k_feats[p][:, c // 2, (c % 2) * T:(c % 2 + 1) * T]
                                last = dve.tensor_scalar(part, part, k_sum[p][:, c:c + 1], None, ALU.mult)
                            last.then_inc(k_normed[p].sem, 1)
                    for p in range(LANES):
                        wait(dve, v_done[p], i)
                        dve_chain[p].link(dve.tensor_tensor(v_rows[p][:], by_row(bank_a[p]),
                                          w["bv"][:].unsqueeze(1).broadcast_to([P, TT, D]), ALU.add))
                        for t in range(TT):
                            last = dve.tensor_scalar(v_rows[p][:, t, :], v_rows[p][:, t, :],
                                                     keep_row[:, bass.ds((i * LANES + p) * TT + t, 1)], None, ALU.mult)
                        last.then_inc(v_ready[p].sem, 1)
                    for p in range(LANES):
                        wait(dve, q_exp[p], i)
                        dve_chain[p].link(dve.tensor_reduce(q_rsum[p][:], by_head(q_rows[p]), AX.X, ALU.add))
                        dve_chain[p].link(dve.reciprocal(q_rsum[p][:], q_rsum[p][:]))
                        if not v_first:
                            wait(dve, k_exp[p], i)
                            dve_chain[p].link(dve.reciprocal(k_sum[p][:], k_sum[p][:]))
                    for p in range(LANES):
                        wait(dve, att_done[p], i)
                        if v_first:
                            dve.tensor_tensor(att[p][:], bank_a[p][:, 0:4 * P].rearrange("p (c e) -> p c e", e=P),
                                              block_mask[:].unsqueeze(1).broadcast_to([P, 2 * FT, P]), ALU.mult)\
                               .then_inc(att_ready[p].sem, 1)
                            continue
                        for b in range(2):
                            for f in range(FT):
                                c = b * FT + f
                                last = dve.scalar_tensor_tensor(att[p][:, c, :], bank_a[p][:, c * P:(c + 1) * P],
                                                                k_sum[p][:, f * 2 + b:f * 2 + b + 1], block_mask[:],
                                                                ALU.mult, ALU.mult)
                        last.then_inc(att_ready[p].sem, 1)
                    for p in range(LANES):
                        wait(dve, y_done[p], i)
                        dve_chain[p].link(dve.tensor_tensor(by_head(y[p]),
                                          by_row(bank_b[p]).rearrange("p t (h e) -> p (t h) e", e=dh),
                                          q_rsum[p][:].unsqueeze(2).broadcast_to([P, TT * heads, dh]), ALU.mult))
                        layer_norm_stats(dve, lambda t: y[p][:, t, :], stats[p], mean_var[p], y_stats[p])
                    for p in range(LANES):
                        wait(dve, y_rstd[p], i)
                        layer_norm_apply(dve, lambda t: y[p][:, t, :], rows[p], mean_var[p], rstd[p], y_normed[p])
                    for p in range(LANES):
                        dve_chain[p].link(dve.tensor_tensor(x_pair(p), x_pair(p),
                                          w["b_out"][:].unsqueeze(1).broadcast_to([P, TT, D]), ALU.add))
                    for p in range(LANES):
                        wait(dve, out_done[p], i)
                        dve.tensor_tensor(x_pair(p), by_row(bank_b[p]), x_pair(p), ALU.add).then_inc(x_ready[p].sem, 1)
                        dve_chain[p].end()
    release_semaphores(nc, used)


Q_SLOTS = (0, 0, 0, 1, 1, 2)
K_SLOTS = (0, 1, 2, 0, 1, 0)
ROWS_QK = 16 * len(Q_SLOTS)
ROWS_MASKED = ROWS_QK + 3
ROWS_SHIFTED = ROWS_MASKED + 3


def softmax_attention(nc, a, keep):
    l, H = 1, 16
    dh = D // H
    HG = 4
    CH = 2 * 2 * (H // HG)
    VW = 32
    used = []
    with ExitStack() as ctx:
        def sb(name, shape, dt=F32):
            return ctx.enter_context(nc.sbuf_tensor(f"{name}_l{l}", shape, dt))

        def ps(name, shape, dt=F32):
            return ctx.enter_context(nc.psum_tensor(f"{name}_l{l}", shape, dt))

        def sem(name):
            return layer_semaphore(nc, used, f"{name}_l{l}")

        def lanes(name, shape, dt=F32):
            return [sb(f"{name}{p}", shape, dt) for p in range(LANES)]

        def signals(name, per=1, start=0):
            return [Signal(sem(f"{name}{p}"), per, start) for p in range(LANES)]

        w, weights_in = keep["w"][l], 16 * len(keep["loads"][l])
        keep_row = sb("keep_row", [P, PAIRS * TT])
        mask = sb("mask", [B, T])
        mask_parts = sb("mask_parts", [B, 3, T], BF16)

        stats = lanes("stats", [P, TT, 6])
        mean_var = lanes("mean_var", [P, TT, 2])
        rstd = lanes("rstd", [P, TT])
        rows = lanes("rows", [P, TT, D])
        feats = lanes("feats", [P, FT, PAIR])
        qk = [[sb(f"{n}{p}", [P, FT, PAIR]) for n in "qk"] for p in range(LANES)]
        part_store = lanes("part_store", [P, 6, FT, PAIR], BF16)
        parts = [[[x[:, 3 * n + j, :, :] for j in range(3)] for n in range(2)] for x in part_store]
        store_f32 = [x[:].rearrange("p j f t -> p (j f t)").bitcast(F32) for x in part_store]
        stack = [[sb(f"{n}_stack{p}", [P, H, PAIR], BF16) for n in "qk"] for p in range(LANES)]
        v_rows = lanes("v_rows", [P, TT, H, VW])
        negmax = lanes("negmax", [P, TT, H])
        negmax_t = [x[0:H, 0, :] for x in feats]
        negmax_parts = [x[0:H, 4:6, :, :].rearrange("p j f t -> p (j f) t")[:, 0:3, :] for x in part_store]
        probs = [[x[:, j * HG * T:(j + 1) * HG * T].rearrange("p (h t) -> p h t", t=T) for j in range(2)]
                 for x in store_f32]
        y_heads = [k[:].rearrange("p f t -> p (f t)").rearrange("p (g t) -> p g t", t=T) for _, k in qk]
        y_rsum = lanes("y_rsum", [P, 2 * H])
        y = [q[:].rearrange("p f t -> p (f t)").rearrange("p (t d) -> p t d", d=D) for q, _ in qk]

        bank_a = [ps(f"bank_a{p}", [P, 2 * 512]) for p in range(LANES)]
        bank_b = [ps(f"bank_b{p}", [P, 2 * 512]) for p in range(LANES)]
        banks = [bank_a, bank_b]

        def by_feat(x):
            return x[:].rearrange("p (f t) -> p f t", f=FT)

        def by_row(x):
            return x[:].rearrange("p (t f) -> p t f", t=TT)

        def by_quad(x):
            return x[:].rearrange("p (h t) -> p h t", h=HG)

        mask_in, keep_in, mask_step, mask_out, filled = (
            sem(s) for s in ("mask_in", "keep_in", "mask_step", "mask_out", "filled"))
        x_stats, x_rstd, x_normed = signals("x_stats"), signals("x_rstd"), signals("x_normed")
        x_turned, feats_ready = signals("x_turned"), signals("feats_ready")
        qk_done, qk_ready = signals("qk_done", 2), signals("qk_ready", 2)
        qk_cast, qk_rest = signals("qk_cast", 4), signals("qk_rest", 4)
        n_stack = 16 * (2 * len(Q_SLOTS) + 1)
        part_out = [signals("q_out", 16), signals("k_out", 16)]
        stack_in = signals("stack_in", n_stack)
        v_done, v_read, v_ready = signals("v_done"), signals("v_read"), signals("v_ready")
        raw_done, max_ready = signals("raw_done", CH), signals("max_ready", CH)
        max_turned, max_split, max_in = signals("max_turned"), signals("max_split"), signals("max_in", 48)
        scores_done, exp_ready, pv_done = signals("scores_done", CH, start=1), signals("exp_ready", CH), signals("pv_done", CH, start=1)
        yh_ready, yh_turned, y_part = signals("yh_ready", 2), signals("yh_turned", 2), signals("y_part", 2)
        y_stats, y_rstd, y_normed = signals("y_stats"), signals("y_rstd"), signals("y_normed")
        h_turned, h_ready, out_done, x_ready = signals("h_turned"), signals("h_ready"), signals("out_done"), signals("x_ready", start=1)
        dve_chain = [Chain(sem(f"dve_chain{p}"), 6) for p in range(LANES)]
        pool_chain = [Chain(sem(f"pool_chain{p}"), 2) for p in range(LANES)]

        def chunk(c):
            b, c = divmod(c, CH // 2)
            g, half = divmod(c, 2)
            return b, half, g

        with nc.Block() as block:
            @block.sync
            def _(sp):
                sp.dma_start(mask[:], a["mask"][l]).then_inc(mask_in, 16)
                sp.dma_start(keep_row[:], a["mask_rows"][l]).then_inc(keep_in, 16)
                sp.wait_ge(mask_step, 5)
                for j in range(3):
                    sp.dma_start(a["mask_dram"][j], mask_parts[:, j, :]).then_inc(mask_out, 16)
                sp.wait_ge(mask_out, 48)
                sp.wait_ge(filled, 4 * LANES)
                with sp.Fori(0, STEPS) as i:
                    for p in range(LANES):
                        wait(sp, scores_done[p], i, 0)
                        sp.dma_start(stack[p][1][ROWS_QK:ROWS_MASKED, :, :],
                                     a["mask_dram"].rearrange("j b t -> j (b t)")[:, bass.ds((i * LANES + p) * PAIR, PAIR)]
                                     .unsqueeze(1).broadcast_to([3, H, PAIR])).then_inc(stack_in[p].sem, 16)
                    for n in range(2):
                        for p in range(LANES):
                            wait(sp, qk_rest[p], i, 2 * n + 2)
                            sp.dma_start(a["part_dram"][p, n].rearrange("j (f e) t -> e j f t", e=P),
                                         part_store[p][:, 3 * n:3 * n + 3, :, :]).then_inc(part_out[n][p].sem, 16)
                    for n, slots in enumerate((Q_SLOTS, K_SLOTS)):
                        for p in range(LANES):
                            wait(sp, part_out[n][p], i, 16)
                            for s, j in enumerate(slots):
                                sp.dma_start(stack[p][n][s * dh:(s + 1) * dh, :, :],
                                             a["part_dram"][p, n, j].rearrange("(h r) t -> r h t", r=dh))\
                                  .then_inc(stack_in[p].sem, 16)
                    for p in range(LANES):
                        wait(sp, max_split[p], i)
                        for j in range(3):
                            sp.dma_start(stack[p][0][ROWS_MASKED + j:ROWS_MASKED + j + 1, :, :],
                                         negmax_parts[p][:, j, :]).then_inc(max_in[p].sem, 16)

            @block.gpsimd
            def _(pool):
                n = 0
                for p in range(LANES):
                    for part, value in ((stack[p][0][ROWS_QK:ROWS_SHIFTED, :, :], 1.0),
                                        (stack[p][1][ROWS_QK:ROWS_SHIFTED, :, :], 1.0),
                                        (v_rows[p][:, :, :, dh:VW], 0.0), (v_rows[p][:, :, :, dh:dh + 1], 1.0)):
                        pool.memset(part, value).then_inc(filled, 1)
                        n += 1
                        pool.wait_ge(filled, n)
                with pool.Fori(0, STEPS) as i:
                    for p in range(LANES):
                        pool_chain[p].begin(pool, i)
                        wait(pool, x_stats[p], i)
                        layer_norm_rstd(pool, pool_chain[p], keep, mean_var[p], rstd[p], x_rstd[p])
                    for p in range(LANES):
                        wait(pool, y_stats[p], i)
                        layer_norm_rstd(pool, pool_chain[p], keep, mean_var[p], rstd[p], y_rstd[p])
                        pool_chain[p].end()

            @block.tensor
            def _(pe):
                for p in range(LANES):
                    pe.sem_inc(scores_done[p].sem, 1)
                    pe.sem_inc(pv_done[p].sem, 1)
                pe.wait_ge(filled, 4 * LANES)
                pe.wait_ge(keep["w_in"][l], weights_in)
                with pe.Fori(0, STEPS) as i:
                    def pv(c, p):
                        b, half, g = chunk(c)
                        wait(pe, exp_ready[p], i, c + 1)
                        if c == CH // 2:
                            wait(pe, yh_ready[p], i, 1)
                        for j in range(HG):
                            last = pe.matmul(bank_b[p][j * VW:(j + 1) * VW, g * T:(g + 1) * T],
                                             v_rows[p][:, 2 * b + half, g * HG + j, :], probs[p][c % 2][:, j, :],
                                             start=(half == 0), stop=(half == 1))
                        last.then_inc(pv_done[p].sem, 1)

                    for p in range(LANES):
                        wait(pe, x_normed[p], i)
                        wait(pe, x_ready[p], i, 0)
                        transpose_rows(pe, keep, by_feat(bank_a[p]), rows[p], x_turned[p])
                    for p in range(LANES):
                        wait(pe, feats_ready[p], i)
                        project_feats(pe, by_feat(bank_b[p]), feats[p], w["q"], qk_done[p])
                        project_feats(pe, by_feat(bank_a[p]), feats[p], w["k"], qk_done[p])
                    for p in range(LANES):
                        wait(pe, qk_ready[p], i, 1)
                        project_rows(pe, by_row(bank_b[p]), feats[p], w["v"], v_done[p])
                    for c in range(CH):
                        b, half, g = chunk(c)
                        for p in range(LANES):
                            if c == 0:
                                wait(pe, stack_in[p], i, n_stack)
                            elif c == 1:
                                wait(pe, v_read[p], i)
                            else:
                                wait(pe, max_ready[p], i, c - 1)
                            for j in range(HG):
                                h, r = g * HG + j, b * T + half * P
                                last = pe.matmul(by_quad(banks[c % 2][p])[:, j, :],
                                                 stack[p][0][0:ROWS_MASKED, h, r:r + P],
                                                 stack[p][1][0:ROWS_MASKED, h, b * T:(b + 1) * T],
                                                 start=True, stop=True)
                            last.then_inc(raw_done[p].sem, 1)
                    for p in range(LANES):
                        wait(pe, max_ready[p], i, CH)
                        for t in range(TT):
                            last = pe.transpose(bank_a[p][0:H, t * P:(t + 1) * P], negmax[p][:, t, :], keep["ident"][:])
                        last.then_inc(max_turned[p].sem, 1)
                    for b in range(2):
                        for c in range(b * CH // 2, (b + 1) * CH // 2):
                            _, half, g = chunk(c)
                            for p in range(LANES):
                                if c == 0:
                                    wait(pe, max_in[p], i, 48)
                                elif c == CH // 2:
                                    wait(pe, y_part[p], i, 1)
                                else:
                                    wait(pe, exp_ready[p], i, c)
                                for j in range(HG):
                                    h, r = g * HG + j, b * T + half * P
                                    last = pe.matmul(by_quad(bank_a[p])[:, j, :],
                                                     stack[p][1][0:ROWS_SHIFTED, h, r:r + P],
                                                     stack[p][0][0:ROWS_SHIFTED, h, b * T:(b + 1) * T],
                                                     start=True, stop=True)
                                last.then_inc(scores_done[p].sem, 1)
                                if c % (CH // 2):
                                    pv(c - 1, p)
                        for p in range(LANES):
                            pv((b + 1) * CH // 2 - 1, p)
                        for p in range(LANES):
                            wait(pe, yh_ready[p], i, b + 1)
                            for t in range(2):
                                for g in range(H // HG):
                                    last = pe.transpose(bank_a[p][:, (t * 4 + g) * P:(t * 4 + g + 1) * P],
                                                        y_heads[p][:, g, t * P:(t + 1) * P], keep["ident"][:])
                            last.then_inc(yh_turned[p].sem, 1)
                    for p in range(LANES):
                        wait(pe, y_normed[p], i)
                        transpose_rows(pe, keep, by_feat(bank_a[p]), rows[p], h_turned[p])
                    for p in range(LANES):
                        wait(pe, h_ready[p], i)
                        project_rows(pe, by_row(bank_b[p]), feats[p], w["out"], out_done[p])

            @block.scalar
            def _(act):
                act.wait_ge(keep["w_in"][l], weights_in)
                with act.Fori(0, STEPS) as i:
                    for p in range(LANES):
                        wait(act, x_turned[p], i)
                        for f in range(FT):
                            last = act.activation(feats[p][:, f, :], by_feat(bank_a[p])[:, f, :], ACT.Identity,
                                                  bias=w["ln_b"][:, f:f + 1], scale=w["ln_w"][:, f:f + 1])
                        last.then_inc(feats_ready[p].sem, 1)
                    for p in range(LANES):
                        for n, (bank, bias) in enumerate(((bank_b, "bq"), (bank_a, "bk"))):
                            wait(act, qk_done[p], i, n + 1)
                            for f in range(FT):
                                last = act.activation(qk[p][n][:, f, :], by_feat(bank[p])[:, f, :], ACT.Identity,
                                                      bias=w[bias][:, f:f + 1])
                            last.then_inc(qk_ready[p].sem, 1)
                    for n in range(2):
                        for p in range(LANES):
                            if n == 0:
                                wait(act, scores_done[p], i, 0)
                            wait(act, qk_ready[p], i, n + 1)
                            act.activation(parts[p][n][0], qk[p][n][:], ACT.Copy).then_inc(qk_cast[p].sem, 1)
                        for p in range(LANES):
                            wait(act, qk_rest[p], i, 2 * n + 1)
                            act.activation(parts[p][n][1], qk[p][n][:], ACT.Copy).then_inc(qk_cast[p].sem, 1)
                    for b in range(2):
                        for c in range(b * CH // 2, (b + 1) * CH // 2):
                            for p in range(LANES):
                                wait(act, scores_done[p], i, c + 1)
                                wait(act, pv_done[p], i, max(c - 1, 0))
                                act.activation(probs[p][c % 2], by_quad(bank_a[p]), ACT.Exp)\
                                   .then_inc(exp_ready[p].sem, 1)
                        for p in range(LANES):
                            wait(act, pv_done[p], i, (b + 1) * CH // 2)
                            act.activation(y_heads[p], by_quad(bank_b[p]), ACT.Copy).then_inc(yh_ready[p].sem, 1)
                    for p in range(LANES):
                        wait(act, h_turned[p], i)
                        silu_modulated(act, keep, l, i * LANES + p, by_feat(bank_a[p]), feats[p], h_ready[p])

            @block.vector
            def _(dve):
                dve.wait_ge(mask_in, 16)
                dve.tensor_scalar(mask[:], mask[:], 1.0, 1e6, ALU.subtract, ALU.mult).then_inc(mask_step, 1)
                dve.wait_ge(mask_step, 1)
                dve.tensor_copy(mask_parts[:, 0, :], mask[:]).then_inc(mask_step, 1)
                dve.wait_ge(mask_step, 2)
                dve.tensor_tensor(mask[:], mask[:], mask_parts[:, 0, :], ALU.subtract).then_inc(mask_step, 1)
                dve.wait_ge(mask_step, 3)
                dve.tensor_copy(mask_parts[:, 1, :], mask[:]).then_inc(mask_step, 1)
                dve.wait_ge(mask_step, 4)
                dve.tensor_tensor(mask_parts[:, 2, :], mask[:], mask_parts[:, 1, :], ALU.subtract).then_inc(mask_step, 1)
                dve.wait_ge(keep_in, 16)
                dve.wait_ge(filled, 4 * LANES)
                for p in range(LANES):
                    dve.sem_inc(x_ready[p].sem, 1)
                dve.wait_ge(keep["w_in"][l], weights_in)
                dve.wait_ge(keep["x_rest_in"], 16 * (PAIRS - LANES))
                with dve.Fori(0, STEPS) as i:
                    def x_tile(p):
                        return lambda t: keep["x"][:, bass.ds((i * LANES + p) * TT + t, 1), :].rearrange("p a d -> p (a d)")

                    def x_pair(p):
                        return keep["x"][:, bass.ds((i * LANES + p) * TT, TT), :]

                    for p in range(LANES):
                        dve_chain[p].begin(dve, i)
                        layer_norm_stats(dve, x_tile(p), stats[p], mean_var[p], x_stats[p])
                    for p in range(LANES):
                        wait(dve, x_rstd[p], i)
                        layer_norm_apply(dve, x_tile(p), rows[p], mean_var[p], rstd[p], x_normed[p])
                    for n in range(2):
                        for p in range(LANES):
                            wait(dve, qk_cast[p], i, 2 * n + 1)
                            dve.tensor_tensor(qk[p][n][:], qk[p][n][:], parts[p][n][0], ALU.subtract)\
                               .then_inc(qk_rest[p].sem, 1)
                        for p in range(LANES):
                            wait(dve, qk_cast[p], i, 2 * n + 2)
                            dve.tensor_tensor(parts[p][n][2], qk[p][n][:], parts[p][n][1], ALU.subtract)\
                               .then_inc(qk_rest[p].sem, 1)
                    for p in range(LANES):
                        wait(dve, v_done[p], i)
                        dve.tensor_tensor(rows[p][:], by_row(bank_b[p]),
                                          w["bv"][:].unsqueeze(1).broadcast_to([P, TT, D]), ALU.add)\
                           .then_inc(v_read[p].sem, 1)
                        wait(dve, v_read[p], i)
                        for t in range(TT):
                            last = dve.tensor_scalar(v_rows[p][:, t, :, 0:dh],
                                                     rows[p][:, t, :].rearrange("p (h e) -> p h e", e=dh),
                                                     keep_row[:, bass.ds((i * LANES + p) * TT + t, 1)], None, ALU.mult)
                        last.then_inc(v_ready[p].sem, 1)
                    for c in range(CH):
                        b, half, g = chunk(c)
                        for p in range(LANES):
                            wait(dve, raw_done[p], i, c + 1)
                            dve.tensor_reduce(negmax[p][:, 2 * b + half, g * HG:(g + 1) * HG], by_quad(banks[c % 2][p]),
                                              AX.X, ALU.max, negate=True).then_inc(max_ready[p].sem, 1)
                    for p in range(LANES):
                        wait(dve, max_turned[p], i)
                        turned, part = bank_a[p][0:H, 0:PAIR], negmax_parts[p]
                        dve_chain[p].link(dve.tensor_copy(part[:, 0, :], turned))
                        dve_chain[p].link(dve.tensor_tensor(negmax_t[p], turned, part[:, 0, :], ALU.subtract))
                        dve_chain[p].link(dve.tensor_copy(part[:, 1, :], negmax_t[p]))
                        dve.tensor_tensor(part[:, 2, :], negmax_t[p], part[:, 1, :], ALU.subtract)\
                           .then_inc(max_split[p].sem, 1)
                    for b in range(2):
                        for p in range(LANES):
                            wait(dve, yh_turned[p], i, b + 1)
                            got = bank_a[p][:].rearrange("p (n e) -> p n e", e=VW)
                            dve_chain[p].link(dve.reciprocal(y_rsum[p][:], got[:, :, dh:dh + 1].rearrange("p n e -> p (n e)")))
                            dve.tensor_tensor(y[p][:, 2 * b:2 * b + 2, :].rearrange("p t (h e) -> p (t h) e", e=dh),
                                              got[:, :, 0:dh], y_rsum[p][:].unsqueeze(2).broadcast_to([P, 2 * H, dh]),
                                              ALU.mult).then_inc(y_part[p].sem, 1)
                    for p in range(LANES):
                        wait(dve, y_part[p], i, 2)
                        layer_norm_stats(dve, lambda t: y[p][:, t, :], stats[p], mean_var[p], y_stats[p])
                    for p in range(LANES):
                        wait(dve, y_rstd[p], i)
                        layer_norm_apply(dve, lambda t: y[p][:, t, :], rows[p], mean_var[p], rstd[p], y_normed[p])
                    for p in range(LANES):
                        dve_chain[p].link(dve.tensor_tensor(x_pair(p), x_pair(p),
                                          w["b_out"][:].unsqueeze(1).broadcast_to([P, TT, D]), ALU.add))
                        dve_chain[p].end()
                    for p in range(LANES):
                        wait(dve, out_done[p], i)
                        dve.tensor_tensor(x_pair(p), by_row(bank_b[p]), x_pair(p), ALU.add).then_inc(x_ready[p].sem, 1)
    release_semaphores(nc, used)


def mamba(nc, a, keep, out):
    l = 3
    DI, N, RANK, TAPS = 2 * D, 16, 64, 4
    MT = DI // P
    NT = 16
    C8 = P // N
    SUB = 32
    XR = RANK + 2 * N
    ND_A, ND_I, ND_H = 4, 4, 4
    LAG = 4

    ORDER = (("dt", "xn", "x0", "x1", "x2", "x3"), ("dt", "z0", "z1", "z2", "z3"), ("dt", "x_dbl", "b", "c"), ("dt",))
    WARM = ("xn", "x0", "x1", "x2", "x3", "z0", "z1", "z2", "z3", "x_dbl", "b", "c", "dt")
    PER_PAIR = sum(map(len, ORDER))

    def use(u, m, name, last=False):
        if isinstance(u, int) and u < 0:
            return WARM.index(name)
        if last:
            return len(WARM) + PER_PAIR * u + m
        return len(WARM) + PER_PAIR * u + sum(map(len, ORDER[:m])) + ORDER[m].index(name)

    used = []
    with ExitStack() as ctx:
        def sb(name, shape, dt=F32):
            return ctx.enter_context(nc.sbuf_tensor(f"{name}_l{l}", shape, dt))

        def ps(name, shape, dt=F32):
            return ctx.enter_context(nc.psum_tensor(f"{name}_l{l}", shape, dt))

        def sem(name):
            return layer_semaphore(nc, used, f"{name}_l{l}")

        w = {"in": sb("in_w", [P, FT, 2 * DI]), "x": sb("x_w", [P, MT, XR]), "dt": sb("dt_w", [XR, DI]),
             "out": sb("out_w", [P, MT, D]), "conv": sb("conv_w", [P, MT, TAPS]), "a_log": sb("a_log", [P, DI // C8]),
             "conv_b": sb("conv_b", [P, MT]), "dt_b": sb("dt_b", [P, MT]), "d": sb("d", [P, MT])}
        decay_rate = sb("decay_rate", [P, DI // C8])
        spread = sb("spread", [3 * SUB, NT // 4, P], BF16)
        gather = sb("gather", [P, NT // 4, SUB])
        spread_bc = sb("spread_bc", [XR, 2, P])

        stats = sb("stats", [P, TT, 6])
        mean_var = sb("mean_var", [P, TT, 2])
        rstd = sb("rstd", [P, TT])
        rows = sb("rows", [P, TT, D])
        feats = sb("feats", [P, FT, PAIR])
        x_pad = sb("x_pad", [P, MT, 2, TAPS - 1 + T])
        x_dbl = sb("x_dbl", [XR, PAIR])
        u_act = [sb(f"u_act{p}", [P, MT, PAIR]) for p in range(2)]
        z_act = [sb(f"z_act{p}", [P, MT, PAIR]) for p in range(2)]
        bc_rep = [[sb(f"{n}_rep{p}", [P, PAIR]) for n in "bc"] for p in range(2)]
        soft = sb("soft", [P, PAIR])
        dt_dtu = sb("dt_dtu", [P, 2, PAIR])
        parts = sb("parts", [P, 3, 2, PAIR], BF16)
        stack = [sb(f"stack{j}", [3 * SUB, 2, 4, PAIR], BF16) for j in range(2)]
        decay = [sb(f"decay{j}", [P, 2, T]) for j in range(ND_A)]
        inflow = [sb(f"inflow{j}", [P, PAIR]) for j in range(ND_I)]
        state = [sb(f"state{j}", [P, PAIR]) for j in range(ND_H)]
        seen = [sb(f"seen{j}", [P, PAIR]) for j in range(ND_H)]
        y_sum = sb("y_sum", [P, PAIR])
        y_gated = [sb(f"y_gated{p}", [P, MT, PAIR]) for p in range(2)]
        gate = [sb(f"gate{p}", [P, 2, D]) for p in range(2)]
        out_rows = sb("out_rows", [P, TT, D])

        dt_bank = [ps(f"dt_bank{j}", [P, PAIR]) for j in range(2)]
        dtu_bank = [ps(f"dtu_bank{j}", [P, PAIR]) for j in range(2)]
        y_bank = [ps(f"y_bank{j}", [P, PAIR]) for j in range(2)]
        front = ps("front", [P, 2 * 512])
        front_bank = [front[:, 0:512], front[:, 512:1024]]

        in_in, w_in, vec_in = sem("in_in"), sem("w_in"), sem("vec_in")
        made, rate_step = sem("made"), sem("rate_step")
        MADE = 11 + ND_A
        front_done, front_read = sem("front_done"), sem("front_read")
        x_stats, x_rstd, x_normed = sem("x_stats"), sem("x_rstd"), sem("x_normed")
        conv_done, act_done, act_step, dve_step, pool_step = (
            sem(n) for n in ("conv_done", "act_done", "act_step", "dve_step", "pool_step"))
        dt_step = sem("dt_step")
        soft_ready, dt_made, part_cast, part_rest, stack_in = (
            sem(n) for n in ("soft_ready", "dt_made", "part_cast", "part_rest", "stack_in"))
        dt_spread, dtu_spread, decay_ready, inflow_ready, state_ready, seen_ready, y_summed = (
            sem(n) for n in ("dt_spread", "dtu_spread", "decay_ready", "inflow_ready", "state_ready", "seen_ready",
                             "y_summed"))
        y_read, y_ready, out_done, out_gated, out_added = (
            sem(n) for n in ("y_read", "y_ready", "out_done", "out_gated", "out_added"))
        gate_in, stored = [sem(f"gate_in{p}") for p in range(2)], sem("stored")
        STACK_DMAS = 12

        def wait(eng, s, value):
            if not (isinstance(value, int) and value <= 0):
                eng.wait_ge(s, value)

        def blocks(eng, body):
            for m in range(MT):
                body(0, 0, m, False)
            with eng.Fori(0, PAIRS // 2 - 1) as i:
                for du in (1, 2):
                    for m in range(MT):
                        body(i * 2 + du, du % 2, m, False)
            for m in range(MT):
                body(PAIRS - 1, 1, m, True)

        def next_block(u, par, m):
            return (u, par, m + 1) if m + 1 < MT else (u + 1, 1 - par, 0)

        def has_next(m, last):
            return not (last and m + 1 == MT)

        with nc.Block() as block:
            @block.sync
            def _(sp):
                def load_gate(u, par):
                    rows = a["gate_dram"][bass.ds(u * 2, 2), :]
                    wait(sp, out_gated, u - 1)
                    sp.dma_start(gate[par][:], rows.rearrange("b d -> (b d)")
                                 .partition_broadcast(P).rearrange("p (b d) -> p b d", b=2)).then_inc(gate_in[par], 16)

                def load_stack(g, j):
                    block_before, halved, split = NT * (g - 1), 2 * g + 1, 2 * g + 2
                    wait(sp, dtu_spread, block_before)
                    for part, (signal, value) in enumerate(((part_cast, halved), (part_cast, split), (part_rest, split))):
                        wait(sp, signal, value)
                        for s in range(4):
                            sp.dma_start(stack[j][part * SUB:(part + 1) * SUB, :, s, :],
                                         parts[s * SUB:(s + 1) * SUB, part, :, :]).then_inc(stack_in, 16)

                def store(u):
                    rows = row_tiles(out)[:, bass.ds(u * TT, TT), :]
                    wait(sp, out_added, u + 1)
                    sp.dma_start(rows, out_rows[:]).then_inc(stored, 16)

                v = a["mamba"]
                sp.dma_start(w["in"][:], k_tiles(v["in"])).then_inc(in_in, 16)
                sp.dma_start(w["x"][:], k_tiles(v["x"])).then_inc(w_in, 16)
                sp.dma_start(w["dt"][0:RANK, :], v["dt"]).then_inc(w_in, 16)
                sp.dma_start(w["out"][:], k_tiles(v["out"])).then_inc(w_in, 16)
                load_stack(0, 0)
                load_gate(0, 0)
                sp.sem_inc(stored, 1)

                def body(u, par, m, last):
                    if has_next(m, last):
                        load_stack(u * MT + m + 1, (m + 1) % 2)
                    if m == 1 and not (isinstance(u, int) and u == 0):
                        store(u - 1)
                    if m == 2 and not last:
                        load_gate(u + 1, 1 - par)

                blocks(sp, body)
                store(PAIRS - 1)
                sp.wait_ge(stored, 16 * PAIRS + 1)

            @block.gpsimd
            def _(pool):
                n = [0]

                def make(ins):
                    n[0] += 1
                    ins.then_inc(made, 1)
                    pool.wait_ge(made, n[0])

                def select(view, base, pattern, op, fill, channel=1):
                    make(pool.affine_select(out=view, in_=view, compare_op=op, fill=fill, base=base,
                                            pattern=pattern, channel_multiplier=channel))

                make(pool.memset(spread[:], 0.0))
                view = spread[:].rearrange("p j (c n) -> p j c n", n=N)
                for part in range(3):
                    select(view, -SUB * part, [[-C8, NT // 4], [-1, C8], [0, N]], ALU.not_equal, 1.0)
                make(pool.memset(gather[:], 1.0))
                select(gather[:], 0, [[N * C8, NT // 4], [-N, SUB]], ALU.is_ge, 0.0)
                select(gather[:], N - 1, [[-N * C8, NT // 4], [N, SUB]], ALU.is_ge, 0.0, channel=-1)
                make(pool.memset(spread_bc[:], 0.0))
                for c in range(2):
                    view = spread_bc[:, c, :].rearrange("p (c n) -> p c n", n=N)
                    select(view, -RANK - N * c, [[0, C8], [-1, N]], ALU.not_equal, 1.0)
                make(pool.memset(w["dt"][RANK:XR, :], 0.0))
                make(pool.memset(x_pad[:, :, :, 0:TAPS - 1], 0.0))
                for j in range(ND_A):
                    make(pool.memset(decay[j][:, :, 0:1], 0.0))

                def rstd_of(u):
                    wait(pool, x_stats, u + 1)
                    pool.tensor_tensor(rstd[:], mean_var[:, :, 1], keep["eps"][:], ALU.add).then_inc(pool_step, 1)
                    wait(pool, pool_step, u + 1)
                    pool.tensor_tensor(rstd[:], rstd[:], keep["half"][:], ALU.pow).then_inc(x_rstd, 1)

                rstd_of(0)

                def body(u, par, m, last):
                    g = u * MT + m
                    for k in range(NT):
                        t = g * NT + k
                        if m == 0 and k == 1 and not last:
                            rstd_of(u + 1)
                        if m == 2 and k == 2 and not (isinstance(u, int) and u == 0):
                            add_x(u - 1)
                        wait(pool, state_ready, t + 1)
                        wait(pool, y_summed, t - ND_H + 1)
                        pool.tensor_tensor(seen[k % ND_H][:], state[k % ND_H][:], bc_rep[par][1][:], ALU.mult)\
                            .then_inc(seen_ready, 1)

                def add_x(u):
                    wait(pool, out_gated, u + 1)
                    pool.tensor_tensor(out_rows[:], out_rows[:], keep["x"][:, bass.ds(u * TT, TT), :], ALU.add)\
                        .then_inc(out_added, 1)

                blocks(pool, body)
                add_x(PAIRS - 1)

            @block.tensor
            def _(pe):
                pe.wait_ge(made, MADE)

                def take(u, m, name, last=False):
                    n = use(u, m, name, last)
                    wait(pe, front_read, n)

                def project_in(u, m, name, bank):
                    take(u, m, name)
                    e = int(name[1]) + (MT if name[0] == "z" else 0)
                    for k in range(FT):
                        last = pe.matmul(front_bank[bank], w["in"][:, k, e * P:(e + 1) * P], feats[:, k, :],
                                         start=(k == 0), stop=(k == FT - 1))
                    last.then_inc(front_done, 1)

                def turn(u):
                    take(u, 0, "xn")
                    wait(pe, x_normed, u + 2)
                    for f in range(FT):
                        for t in range(TT):
                            last = pe.transpose(front[:, f * 512 + t * P:f * 512 + (t + 1) * P],
                                                rows[:, t, f * P:(f + 1) * P], keep["ident"][:])
                    last.then_inc(front_done, 1)

                def project_dbl(u, par):
                    take(u, 2, "x_dbl")
                    wait(pe, act_done, 2 * (u + 2))
                    for k in range(MT):
                        last = pe.matmul(front_bank[1][0:XR, :], w["x"][:, k, :], u_act[par][:, k, :],
                                         start=(k == 0), stop=(k == MT - 1))
                    last.then_inc(front_done, 1)

                def repeat(u, c):
                    take(u, 2, "bc"[c])
                    pe.matmul(front_bank[c], spread_bc[:, c, :], x_dbl[:], start=True, stop=True).then_inc(front_done, 1)

                def project_dt(u, m, last, target):
                    take(u, m, "dt", last)
                    if m == 2:
                        wait(pe, out_gated, u)
                    pe.matmul(front_bank[0], w["dt"][:, target * P:(target + 1) * P], x_dbl[:],
                              start=True, stop=True).then_inc(front_done, 1)

                def spread_tile(t, j, k):
                    s, i = k % 4, k // 4
                    wait(pe, decay_ready, t - 1)
                    pe.matmul(dt_bank[k % 2][:], spread[:, i, :], stack[j][:, 0, s, :], start=True, stop=True)\
                      .then_inc(dt_spread, 1)
                    wait(pe, inflow_ready, t - 1)
                    pe.matmul(dtu_bank[k % 2][:], spread[:, i, :], stack[j][:, 1, s, :], start=True, stop=True)\
                      .then_inc(dtu_spread, 1)

                def sum_tile(g, j, k):
                    s, i = k % 4, k // 4
                    t = g * NT + k
                    wait(pe, seen_ready, t + 1)
                    if k == 0:
                        wait(pe, y_read, g - 1)
                    pe.matmul(y_bank[j][s * SUB:(s + 1) * SUB, :], gather[:, i, :], seen[k % ND_H][:],
                              start=(i == 0), stop=(i == 3), skip_group_check=True).then_inc(y_summed, 1)

                def project_out(u, par, t):
                    wait(pe, y_ready, MT * (u + 1))
                    for k in range(MT):
                        last = pe.matmul(front[:, t * D:(t + 1) * D], y_gated[par][:, k, t * P:(t + 1) * P],
                                         w["out"][:, k, :], start=(k == 0), stop=(k == MT - 1))
                    last.then_inc(out_done, 1)

                turn(-1)
                pe.wait_ge(in_in, 16)
                for n in range(MT):
                    project_in(-1, 0, f"x{n}", (n + 1) % 2)
                for n in range(MT):
                    project_in(-1, 1, f"z{n}", (n + 1) % 2)
                pe.wait_ge(w_in, 16 * 3)
                project_dbl(-1, 0)
                repeat(-1, 0)
                repeat(-1, 1)
                project_dt(-1, 3, False, 0)

                def body(u, par, m, last):
                    g = u * MT + m
                    for k in range(NT):
                        if k == 0:
                            wait(pe, stack_in, 16 * STACK_DMAS * (g + 1))
                        spread_tile(g * NT + k, m % 2, k)
                        if k >= LAG:
                            sum_tile(g, m % 2, k - LAG)
                        elif not (isinstance(g, int) and g == 0):
                            sum_tile(g - 1, (m + 1) % 2, NT + k - LAG)
                        if k == 0 and has_next(m, last):
                            project_dt(u, m, last, (m + 1) % MT)
                        if m == 0 and not last:
                            if k == 4:
                                turn(u)
                            if k in (6, 8, 10, 12):
                                n = (k - 6) // 2
                                project_in(u, 0, f"x{n}", (n + 1) % 2)
                        if m == 1 and not last and k in (3, 5, 7, 9):
                            n = (k - 3) // 2
                            project_in(u, 1, f"z{n}", (n + 1) % 2)
                        if m == 1 and k in (11, 12, 13, 14) and not (isinstance(u, int) and u == 0):
                            if k == 11:
                                wait(pe, front_read, use(u, 1, "z3") + 1 if not last else use(u, 1, "dt", True) + 1)
                            project_out(u - 1, 1 - par, k - 11)
                        if m == 2 and not last:
                            if k == 3:
                                project_dbl(u, 1 - par)
                            if k == 6:
                                repeat(u, 0)
                            if k == 8:
                                repeat(u, 1)

                blocks(pe, body)
                g = PAIRS * MT
                for k in range(NT - LAG, NT):
                    sum_tile(g - 1, 1, k)
                for t in range(TT):
                    project_out(PAIRS - 1, 1, t)

            @block.scalar
            def _(act):
                for n in ("conv", "a_log", "conv_b", "dt_b", "d"):
                    act.dma_start(w[n][:], a["mamba"][n]).then_inc(vec_in, 16)
                act.wait_ge(vec_in, 16 * 5)
                act.activation(decay_rate[:], w["a_log"][:], ACT.Exp).then_inc(rate_step, 1)

                def got(u, m, name, last=False):
                    wait(act, front_done, use(u, m, name, last) + 1)

                def norm_feats(u):
                    got(u, 0, "xn")
                    for f in range(FT):
                        for b in range(2):
                            e = (u + 1) * 2 + b
                            last = act.activation(feats[:, f, b * T:(b + 1) * T],
                                                  front[:, f * 512 + b * T:f * 512 + (b + 1) * T], ACT.Identity,
                                                  bias=keep["mod_shift"][l][:, f, bass.ds(e, 1)],
                                                  scale=keep["mod_scale"][l][:, f, bass.ds(e, 1)])
                    last.then_inc(front_read, 1)

                def take_x(u, n, par):
                    got(u, 0, f"x{n}")
                    bank = front_bank[(n + 1) % 2]
                    act.activation(x_pad[:, n, :, TAPS - 1:TAPS - 1 + T], bank.rearrange("p (b t) -> p b t", b=2), ACT.Copy)
                    act.activation(u_act[par][:, n, :], bank, ACT.Identity, bias=w["conv_b"][:, n:n + 1],
                                   scale=w["conv"][:, n, TAPS - 1:TAPS]).then_inc(front_read, 1)

                def take_z(u, n, par):
                    got(u, 1, f"z{n}")
                    act.activation(z_act[par][:, n, :], front_bank[(n + 1) % 2], ACT.Copy).then_inc(front_read, 1)

                def silus(u, par):
                    wait(act, conv_done, MT * (u + 2))
                    act.activation(u_act[par][:], u_act[par][:], ACT.Silu).then_inc(act_done, 1)
                    wait(act, front_read, use(u, 1, "z3") + 1)
                    act.activation(z_act[par][:], z_act[par][:], ACT.Silu).then_inc(act_done, 1)

                def take_dbl(u):
                    got(u, 2, "x_dbl")
                    act.activation(x_dbl[:], front_bank[1][0:XR, :], ACT.Copy).then_inc(front_read, 1)

                def take_rep(u, c, par):
                    got(u, 2, "bc"[c])
                    act.activation(bc_rep[par][c][:], front_bank[c], ACT.Copy).then_inc(front_read, 1)

                def soft_a(u, m, last, g, target):
                    got(u, m, "dt", last)
                    wait(act, dt_made, g)
                    wait(act, part_rest, 2 * g)
                    bias = w["dt_b"][:, target:target + 1]
                    act.activation(soft[:], front_bank[0], ACT.Abs, bias=bias).then_inc(act_step, 1)
                    act.activation(dt_dtu[:, 0, :], front_bank[0], ACT.Relu, bias=bias).then_inc(front_read, 1)

                def soft_b(g):
                    wait(act, act_step, 2 * g + 1)
                    act.activation(soft[:], soft[:], ACT.Exp, scale=-1.0).then_inc(act_step, 1)

                def soft_c(g):
                    wait(act, act_step, 2 * g + 2)
                    act.activation(soft[:], soft[:], ACT.Ln, bias=1.0).then_inc(soft_ready, 1)

                def cast_0(g):
                    wait(act, dt_made, g + 1)
                    wait(act, stack_in, 16 * STACK_DMAS * g)
                    act.activation(parts[:, 0, :, :], dt_dtu[:], ACT.Copy).then_inc(part_cast, 1)

                def cast_1(g):
                    wait(act, part_rest, 2 * g + 1)
                    act.activation(parts[:, 1, :, :], dt_dtu[:], ACT.Copy).then_inc(part_cast, 1)

                act.wait_ge(made, MADE)
                norm_feats(-1)
                for n in range(MT):
                    take_x(-1, n, 0)
                for n in range(MT):
                    take_z(-1, n, 0)
                silus(-1, 0)
                take_dbl(-1)
                take_rep(-1, 0, 0)
                take_rep(-1, 1, 0)
                soft_a(-1, 3, False, 0, 0)
                soft_b(0)
                soft_c(0)
                cast_0(0)
                cast_1(0)
                act.wait_ge(rate_step, 2)

                def body(u, par, m, last):
                    g = u * MT + m
                    for k in range(NT):
                        t = g * NT + k
                        tile = m * NT + (k % 4) * 4 + k // 4
                        wait(act, dt_spread, t + 1)
                        wait(act, state_ready, t - ND_A + 1)
                        act.activation(decay[k % ND_A][:, :, 1:T],
                                       dt_bank[k % 2][:].rearrange("p (b t) -> p b t", b=2)[:, :, 1:T], ACT.Exp,
                                       scale=decay_rate[:, tile:tile + 1]).then_inc(decay_ready, 1)
                        if has_next(m, last):
                            if k == 1:
                                soft_a(u, m, last, g + 1, (m + 1) % MT)
                            if k == 2:
                                soft_b(g + 1)
                            if k == 3:
                                soft_c(g + 1)
                            if k == 6:
                                cast_0(g + 1)
                            if k == 8:
                                cast_1(g + 1)
                        if last:
                            continue
                        if m == 0 and k == 5:
                            norm_feats(u)
                        if m == 0 and k in (7, 9, 11, 13):
                            take_x(u, (k - 7) // 2, 1 - par)
                        if m == 1 and k in (4, 6, 8, 10):
                            take_z(u, (k - 4) // 2, 1 - par)
                        if m == 1 and k == 12:
                            silus(u, 1 - par)
                        if m == 2 and k == 4:
                            take_dbl(u)
                        if m == 2 and k in (7, 9):
                            take_rep(u, (k - 7) // 2, 1 - par)

                blocks(act, body)

            @block.vector
            def _(dve):
                dve.wait_ge(rate_step, 1)
                dve.tensor_scalar(decay_rate[:], decay_rate[:], -1.0, None, ALU.mult).then_inc(rate_step, 1)
                dve.wait_ge(made, MADE)

                def x_tile(u):
                    return lambda t: keep["x"][:, bass.ds(u * TT + t, 1), :].rearrange("p a d -> p (a d)")

                def norm_a(u):
                    for t in range(TT):
                        dve.bn_stats(stats[:, t, :], x_tile(u)(t))
                    dve.drain()
                    for t in range(TT):
                        last = dve.bn_aggr(mean_var[:, t, :], stats[:, t, :])
                    last.then_inc(x_stats, 1)

                def norm_b(u):
                    wait(dve, x_rstd, u + 1)
                    for t in range(TT):
                        last = dve.tensor_scalar(rows[:, t, :], x_tile(u)(t), mean_var[:, t, 0:1], rstd[:, t:t + 1],
                                                 ALU.subtract, ALU.mult)
                    last.then_inc(x_normed, 1)

                def conv_tap(u, n, par, tap):
                    if tap == 0:
                        wait(dve, front_read, use(u - 1, 0, f"x{n}") + 1)
                    else:
                        wait(dve, dve_step, (u * MT + n) * 2 + tap)
                    view = u_act[par][:, n, :].rearrange("p (b t) -> p b t", b=2)
                    ins = dve.scalar_tensor_tensor(view, x_pad[:, n, :, tap:tap + T], w["conv"][:, n, tap:tap + 1], view,
                                                   ALU.mult, ALU.add)
                    ins.then_inc(*((conv_done, 1) if tap == TAPS - 2 else (dve_step, 1)))

                def make_dt(g):
                    wait(dve, soft_ready, g + 1)
                    dve.tensor_tensor(dt_dtu[:, 0, :], dt_dtu[:, 0, :], soft[:], ALU.add).then_inc(dt_step, 1)

                def make_dtu(g, par, m):
                    wait(dve, dt_step, g + 1)
                    dve.tensor_tensor(dt_dtu[:, 1, :], dt_dtu[:, 0, :], u_act[par][:, m, :], ALU.mult).then_inc(dt_made, 1)

                def rest_0(g):
                    wait(dve, part_cast, 2 * g + 1)
                    dve.tensor_tensor(dt_dtu[:], dt_dtu[:], parts[:, 0, :, :], ALU.subtract).then_inc(part_rest, 1)

                def rest_1(g):
                    wait(dve, part_cast, 2 * g + 2)
                    dve.tensor_tensor(parts[:, 2, :, :], dt_dtu[:], parts[:, 1, :, :], ALU.subtract).then_inc(part_rest, 1)

                def scan_tile(t, k):
                    wait(dve, decay_ready, t + 1)
                    wait(dve, inflow_ready, t + 1)
                    wait(dve, seen_ready, t - ND_H + 1)
                    dve.tensor_tensor_scan(state[k % ND_H][:], decay[k % ND_A][:].rearrange("p b t -> p (b t)"),
                                           inflow[k % ND_I][:], 0.0, ALU.mult, ALU.add).then_inc(state_ready, 1)

                def finish_y(g, par, m):
                    wait(dve, y_summed, NT * (g + 1))
                    dve.scalar_tensor_tensor(y_sum[:], u_act[par][:, m, :], w["d"][:, m:m + 1], y_bank[m % 2][:],
                                             ALU.mult, ALU.add).then_inc(y_read, 1)

                def finish_y2(g, par, m):
                    wait(dve, y_read, g + 1)
                    dve.tensor_tensor(y_gated[par][:, m, :], y_sum[:], z_act[par][:, m, :], ALU.mult).then_inc(y_ready, 1)

                def gate_out(u, par, gate_value):
                    wait(dve, out_done, TT * (u + 1))
                    wait(dve, stored, 16 * u + 1)
                    wait(dve, gate_in[par], gate_value)
                    for b in range(2):
                        last = dve.tensor_tensor(out_rows[:, 2 * b:2 * b + 2, :],
                                                 front[:, b * 512:(b + 1) * 512].rearrange("p (t d) -> p t d", d=D),
                                                 gate[par][:, b:b + 1, :].broadcast_to([P, 2, D]), ALU.mult)
                    last.then_inc(out_gated, 1)

                norm_a(0)
                norm_b(0)
                for n in range(MT):
                    for tap in range(TAPS - 1):
                        conv_tap(0, n, 0, tap)
                make_dt(0)
                wait(dve, act_done, 2)
                make_dtu(0, 0, 0)
                rest_0(0)
                rest_1(0)

                def body(u, par, m, last):
                    g = u * MT + m
                    first = isinstance(g, int) and g == 0
                    for k in range(NT):
                        t = g * NT + k
                        wait(dve, dtu_spread, t + 1)
                        wait(dve, state_ready, t - ND_I + 1)
                        dve.tensor_tensor(inflow[k % ND_I][:], dtu_bank[k % 2][:], bc_rep[par][0][:], ALU.mult)\
                           .then_inc(inflow_ready, 1)
                        if not (first and k == 0):
                            scan_tile(t - 1, (k - 1) % NT)
                        if k == 5 and not first:
                            pm = (m - 1) % MT
                            finish_y(g - 1, par if m else 1 - par, pm)
                        if k == 6 and not first:
                            finish_y2(g - 1, par if m else 1 - par, (m - 1) % MT)
                        if has_next(m, last):
                            nu, npar, nm = next_block(u, par, m)
                            if k == 4:
                                make_dt(g + 1)
                            if k == 5:
                                make_dtu(g + 1, npar, nm)
                            if k == 7:
                                rest_0(g + 1)
                            if k == 9:
                                rest_1(g + 1)
                        if m == 1 and k == 15 and not (isinstance(u, int) and u == 0):
                            gate_out(u - 1, 1 - par, GATE(u - 1, 1 - par))
                        if last:
                            continue
                        if m == 0 and k == 0:
                            norm_a(u + 1)
                        if m == 0 and k == 2:
                            norm_b(u + 1)
                        if m == 0 and k in (9, 11, 13, 15):
                            for tap in range(TAPS - 1):
                                conv_tap(u + 1, (k - 9) // 2, 1 - par, tap)

                def GATE(u, par):
                    return (u - par) * 8 + 16

                blocks(dve, body)
                scan_tile(PAIRS * MT * NT - 1, NT - 1)
                finish_y(PAIRS * MT - 1, 1, MT - 1)
                finish_y2(PAIRS * MT - 1, 1, MT - 1)
                gate_out(PAIRS - 1, 1, GATE(PAIRS - 1, 1))
    release_semaphores(nc, used)


def network(nc, a, out):
    with ExitStack() as ctx:
        def sb(name, shape, dt=F32):
            return ctx.enter_context(nc.sbuf_tensor(name, shape, dt))

        keep = {"x": sb("x_rows", [P, PAIRS * TT, D]), "half": sb("half", [P, TT]), "eps": sb("eps", [P, TT]),
                "ident": sb("ident", [P, P]),
                "mod_scale": [sb(f"mod_scale{l}", [P, FT, B]) for l in range(4)],
                "mod_shift": [sb(f"mod_shift{l}", [P, FT, B]) for l in range(4)], "w": [{} for _ in range(3)]}
        loads = keep["loads"] = [[] for _ in range(3)]
        keep["w_in"] = [ctx.enter_context(nc.semaphore(f"w_in{l}")) for l in range(3)]
        keep["x_rest_in"] = ctx.enter_context(nc.semaphore("x_rest_in"))

        def load(scope, l, name, shape, src):
            keep["w"][l][name] = t = scope.enter_context(nc.sbuf_tensor(f"{name}_w{l}", shape, F32))
            loads[l].append((t[:], src))

        with ExitStack() as attention:
            for l in range(3):
                v = a["layer"][l]
                load(attention, l, "ln_w", [P, FT], v["ln_w"])
                load(attention, l, "ln_b", [P, FT], v["ln_b"])
                for m in "qkv":
                    load(attention, l, m, [P, FT, D], k_tiles(v[m]))
                load(attention, l, "out", [P, FT, D], k_tiles(v["out"]))
                load(attention, l, "bk", [P, FT], v["bk"])
                if l == 1:
                    load(attention, l, "bq", [P, FT], v["bq"])
                else:
                    load(attention, l, "bq", [P, D], v["bq"].partition_broadcast(P))
                load(attention, l, "bv", [P, D], v["bv"].partition_broadcast(P))
                load(attention, l, "b_out", [P, D], v["b_out"].partition_broadcast(P))
            setup(nc, a, keep)
            linear_attention(nc, a, keep, 0, 8)
            softmax_attention(nc, a, keep)
            linear_attention(nc, a, keep, 2, 16)
        mamba(nc, a, keep, out)


def kernel(**inputs):
    import numpy as np
    import concourse.bacc as bacc
    from concourse.bass_utils import run_bass_kernel_spmd

    nc = bacc.Bacc("TRN2", target_bir_lowering=False, num_devices=1)
    arrays = {}

    def given_as(name, v):
        arrays[name] = v = np.ascontiguousarray(v)
        return nc.dram_tensor(name, v.shape, mybir.dt.from_np(v.dtype), kind="ExternalInput").ap()

    def dram(name, transposed=False):
        v = np.asarray(inputs[name])
        return given_as(name, v.T if transposed else v)

    def columns(name):
        return given_as(name + "_columns", np.asarray(inputs[name]).reshape(-1, P).T)

    a = {
        "x": dram("x"),
        "cond_t": dram("cond_2048", True),
        "mask": [dram("mask_BxSx1_fk1").rearrange("b t o -> b (t o)"), dram("mask_BxS_ff1"), dram("mask_BxS_ik0")],
        "emb_w": [dram("L0_cond_W_emb"), dram("L1_cond_emb_w"), dram("L2_cond_film_emb_W"), dram("L3_cond_ada_w", True)],
        "mask_rows": [columns("mask_BxSx1_fk1"), columns("mask_BxS_ff1"), columns("mask_BxS_ik0")],
        "emb_b": [columns(n) for n in ("L0_cond_b_emb", "L1_cond_emb_b", "L2_cond_film_emb_b", "L3_cond_ada_b")],
        "gate_b": dram("L3_cond_ada_b")[2 * D:3 * D],
        "mod_w": [columns(n) for n in ("L0_cond_ln2_w", "L1_cond_sb_norm_w", "L2_cond_film_norm_scale", "L3_cond_ln_g")],
        "mod_b": [columns(n) for n in ("L0_cond_ln2_b", "L1_cond_sb_norm_b", "L2_cond_film_norm_bias", "L3_cond_ln_b")],
        "part_dram": nc.dram_tensor("qk_parts", (LANES, 2, 3, D, PAIR), BF16).ap(),
        "mask_dram": nc.dram_tensor("mask_parts", (3, B, T), BF16).ap(),
        "gate_dram": nc.dram_tensor("gate_rows", (B, D), F32).ap(),
    }
    names = ("ln_w", "ln_b", "q", "bq", "k", "bk", "v", "bv", "out", "b_out")
    given = (
        ("ln_w", "ln_b", "Wq", "bq", "Wk", "bk", "Wv", "bv", "W_out", "b_out"),
        ("norm_w", "norm_b", "q_w", "q_b", "k_w", "k_b", "v_w", "v_b", "out_w", "out_b"),
        ("norm_scale", "norm_bias", "Wq", "bq", "Wk", "bk", "Wv", "bv", "film_out_W", "film_out_b"),
    )
    by_column = [("ln_w", "ln_b", "bk"), ("ln_w", "ln_b", "bq", "bk"), ("ln_w", "ln_b", "bk")]
    a["layer"] = [{n: (columns if n in by_column[l] else dram)(f"L{l}_cond_{g}") for n, g in zip(names, given[l])}
                  for l in range(3)]
    a["mamba"] = {
        "in": dram("L3_cond_in_proj_w", True), "x": dram("L3_cond_x_proj_w", True), "dt": dram("L3_cond_dt_proj_w", True),
        "out": dram("L3_cond_out_proj_w", True), "conv_b": columns("L3_cond_conv_b"), "dt_b": columns("L3_cond_dt_proj_b"),
        "d": columns("L3_cond_D_param"),
        "conv": given_as("conv_taps", np.asarray(inputs["L3_cond_conv_w"]).reshape(-1, P, 4).transpose(1, 0, 2)),
        "a_log": given_as("a_log_tiles", np.asarray(inputs["L3_cond_A_log"]).reshape(-1, P).T),
    }
    out = nc.dram_tensor("out", (B, T, D), F32, kind="ExternalOutput").ap()
    network(nc, a, out)
    r = run_bass_kernel_spmd(nc, [arrays], core_ids=[0])
    return r.results[0]["out"]
```
